# Optimizing a Trainium2 kernel written in Bass

```python
import numpy as np
import jax
import jax.numpy as jnp

def _softmax(x, axis=-1):
    return jax.nn.softmax(x, axis=axis)

def _gelu(x):
    return jax.nn.gelu(x, approximate=True)

def _silu(x):
    return jax.nn.silu(x)

def _sigmoid(x):
    return jax.nn.sigmoid(x)

def _layernorm(x, axis=-1, eps=1e-05):
    m = jnp.mean(x, axis=axis, keepdims=True)
    v = jnp.var(x, axis=axis, keepdims=True)
    return (x - m) / jnp.sqrt(v + eps)

def _scatter_add(tgt, idx, src, axis=0):
    return tgt.at[idx].add(src)

def _segment_sum(src, seg, n):
    return jax.ops.segment_sum(src, seg, n)
kernel_name = 'mk_hybrid_d1_jaxref_r8_e5d653'

def setup_inputs(seed: int=0):
    np.random.seed(seed)
    _w = jnp.asarray

    def _L0_attn_a_setup():
        import jax, jax.numpy as jnp
        import numpy as np
        D_MODEL = 128
        N_HEADS = 16
        D_HEAD = D_MODEL // N_HEADS
        M_SLOPE = 0.5
        BATCH = 2
        SEQ = 256

        def _alibi_bias(n_heads, seq_len, m, dtype):
            slopes = m ** jnp.arange(n_heads, dtype=dtype)
            pos = jnp.arange(seq_len, dtype=dtype)
            dist = jnp.abs(pos[:, None] - pos[None, :])
            return -dist[None, :, :] * slopes[:, None, None]
        key = jax.random.key(seed)
        k1, k2, k3 = jax.random.split(key, 3)
        x = jax.random.normal(k1, (BATCH, SEQ, D_MODEL), dtype=jnp.float32)
        qkv_w = jax.random.normal(k2, (3 * D_MODEL, D_MODEL), dtype=jnp.float32) * (1.0 / np.sqrt(D_MODEL))
        qkv_b = jnp.zeros((3 * D_MODEL,), dtype=jnp.float32)
        out_w = jax.random.normal(k3, (D_MODEL, D_MODEL), dtype=jnp.float32) * (1.0 / np.sqrt(D_MODEL))
        out_b = jnp.zeros((D_MODEL,), dtype=jnp.float32)
        return {'x': x, 'qkv_w': qkv_w, 'qkv_b': qkv_b, 'out_w': out_w, 'out_b': out_b}
    _L0_attn_a_in = _L0_attn_a_setup()

    def _L0_attn_b_setup():
        import jax, jax.numpy as jnp
        import numpy as np
        import math
        B, T, C = (2, 256, 128)
        H, L = (16, 64)
        DH = C // H
        DHE = DH // 2
        THETA = 10000.0

        def _rope_cache(t, dim):
            inv_freq = 1.0 / THETA ** (jnp.arange(0, dim, 2, dtype=jnp.float32) / dim)
            freqs = jnp.arange(t, dtype=jnp.float32)[:, None] * inv_freq[None, :]
            emb = jnp.concatenate((freqs, freqs), axis=-1)
            return (jnp.cos(emb), jnp.sin(emb))

        def _apply_rope(x, cos, sin):
            x1 = x[..., 0::2]
            x2 = x[..., 1::2]
            rot = jnp.stack((-x2, x1), axis=-1).reshape(x.shape)
            return x * cos[None, None] + rot * sin[None, None]
        key = jax.random.key(seed)
        ks = jax.random.split(key, 10)
        s = 0.02
        return {'x': jax.random.normal(ks[0], (B, T, C), jnp.float32), 'Wq_down': jax.random.normal(ks[1], (C, H * L), jnp.float32) * s, 'Wk_down': jax.random.normal(ks[2], (C, H * L), jnp.float32) * s, 'Wv_down': jax.random.normal(ks[3], (C, H * L), jnp.float32) * s, 'Wq_up_c': jax.random.normal(ks[4], (L, DHE), jnp.float32) * s, 'Wq_up_e': jax.random.normal(ks[5], (L, DHE), jnp.float32) * s, 'Wk_up_c': jax.random.normal(ks[6], (L, DHE), jnp.float32) * s, 'Wk_up_e': jax.random.normal(ks[7], (L, DHE), jnp.float32) * s, 'Wv_up': jax.random.normal(ks[8], (L, DH), jnp.float32) * s, 'Wc': jax.random.normal(ks[9], (C, C), jnp.float32) * s}
    _L0_attn_b_in = _L0_attn_b_setup()

    def _L0_ffn_setup():
        import jax, jax.numpy as jnp
        import numpy as np
        D_MODEL = 128
        EXPANSION = 4
        D_HIDDEN = D_MODEL * EXPANSION
        NUM_STAGES = int(np.log2(D_HIDDEN))

        def butterfly(y, weights, dim):
            lead = y.shape[:-1]
            for stage in range(weights.shape[0]):
                s = 2 ** stage
                nb = dim // (2 * s)
                yr = y.reshape(*lead, nb, 2, s)
                a = yr[..., 0, :]
                b = yr[..., 1, :]
                w = weights[stage].reshape(nb, s, 2, 2)
                na = w[..., 0, 0] * a + w[..., 0, 1] * b
                nb2 = w[..., 1, 0] * a + w[..., 1, 1] * b
                y = jnp.stack([na, nb2], axis=-2).reshape(*lead, dim)
            return y
        key = jax.random.key(seed)
        ks = jax.random.split(key, 6)
        B, S = (4, 256)
        x = jax.random.normal(ks[0], (B, S, D_MODEL), jnp.float32)
        W_exp = jax.random.normal(ks[1], (D_MODEL, D_HIDDEN), jnp.float32) * 0.02
        b_exp = jnp.zeros((D_HIDDEN,), jnp.float32)
        up_weights = jax.random.normal(ks[2], (NUM_STAGES, D_HIDDEN // 2, 2, 2), jnp.float32) * 0.02
        up_bias = jnp.zeros((D_HIDDEN,), jnp.float32)
        down_weights = jax.random.normal(ks[3], (NUM_STAGES, D_HIDDEN // 2, 2, 2), jnp.float32) * 0.02
        W_con = jax.random.normal(ks[4], (D_HIDDEN, D_MODEL), jnp.float32) * 0.02
        b_con = jnp.zeros((D_MODEL,), jnp.float32)
        down_bias = jnp.zeros((D_MODEL,), jnp.float32)
        return dict(x=x, W_exp=W_exp, b_exp=b_exp, up_weights=up_weights, up_bias=up_bias, down_weights=down_weights, W_con=W_con, b_con=b_con, down_bias=down_bias)
    _L0_ffn_in = _L0_ffn_setup()
    _d = {'L0_attn_a_x': _L0_attn_a_in['x'], 'L0_attn_a_qkv_w': _L0_attn_a_in['qkv_w'], 'L0_attn_a_qkv_b': _L0_attn_a_in['qkv_b'], 'L0_attn_a_out_w': _L0_attn_a_in['out_w'], 'L0_attn_a_out_b': _L0_attn_a_in['out_b'], 'L0_attn_b_Wq_down': _L0_attn_b_in['Wq_down'], 'L0_attn_b_Wk_down': _L0_attn_b_in['Wk_down'], 'L0_attn_b_Wv_down': _L0_attn_b_in['Wv_down'], 'L0_attn_b_Wq_up_c': _L0_attn_b_in['Wq_up_c'], 'L0_attn_b_Wq_up_e': _L0_attn_b_in['Wq_up_e'], 'L0_attn_b_Wk_up_c': _L0_attn_b_in['Wk_up_c'], 'L0_attn_b_Wk_up_e': _L0_attn_b_in['Wk_up_e'], 'L0_attn_b_Wv_up': _L0_attn_b_in['Wv_up'], 'L0_attn_b_Wc': _L0_attn_b_in['Wc'], 'L0_ffn_W_exp': _L0_ffn_in['W_exp'], 'L0_ffn_b_exp': _L0_ffn_in['b_exp'], 'L0_ffn_up_weights': _L0_ffn_in['up_weights'], 'L0_ffn_up_bias': _L0_ffn_in['up_bias'], 'L0_ffn_down_weights': _L0_ffn_in['down_weights'], 'L0_ffn_W_con': _L0_ffn_in['W_con'], 'L0_ffn_b_con': _L0_ffn_in['b_con'], 'L0_ffn_down_bias': _L0_ffn_in['down_bias']}
    _x0 = _d['L0_attn_a_x']
    _d['L0_attn_a_x'] = jax.random.normal(jax.random.fold_in(jax.random.key(seed), 1), (4, 1024, 128), dtype=_x0.dtype)
    del _x0
    return _d

def reference(L0_attn_a_x, L0_attn_a_qkv_w, L0_attn_a_qkv_b, L0_attn_a_out_w, L0_attn_a_out_b, L0_attn_b_Wq_down, L0_attn_b_Wk_down, L0_attn_b_Wv_down, L0_attn_b_Wq_up_c, L0_attn_b_Wq_up_e, L0_attn_b_Wk_up_c, L0_attn_b_Wk_up_e, L0_attn_b_Wv_up, L0_attn_b_Wc, L0_ffn_W_exp, L0_ffn_b_exp, L0_ffn_up_weights, L0_ffn_up_bias, L0_ffn_down_weights, L0_ffn_W_con, L0_ffn_b_con, L0_ffn_down_bias):

    def _L0_attn_a_ref(x, qkv_w, qkv_b, out_w, out_b):
        import jax, jax.numpy as jnp
        import numpy as np
        D_MODEL = 128
        N_HEADS = 16
        D_HEAD = D_MODEL // N_HEADS
        M_SLOPE = 0.5
        BATCH = 2
        SEQ = 256

        def _alibi_bias(n_heads, seq_len, m, dtype):
            slopes = m ** jnp.arange(n_heads, dtype=dtype)
            pos = jnp.arange(seq_len, dtype=dtype)
            dist = jnp.abs(pos[:, None] - pos[None, :])
            return -dist[None, :, :] * slopes[:, None, None]
        batch, seq_len, d_model = x.shape
        qkv = x @ qkv_w.T + qkv_b
        qkv = qkv.reshape(batch, seq_len, N_HEADS, 3 * D_HEAD).transpose(0, 2, 1, 3)
        q, k, v = jnp.split(qkv, 3, axis=-1)
        scale = jnp.sqrt(jnp.asarray(D_HEAD, dtype=x.dtype))
        scores = jnp.einsum('bhid,bhjd->bhij', q, k) / scale
        scores = scores + _alibi_bias(N_HEADS, seq_len, M_SLOPE, x.dtype)[None]
        attn = jax.nn.softmax(scores, axis=-1)
        out = jnp.einsum('bhij,bhjd->bhid', attn, v)
        out = out.transpose(0, 2, 1, 3).reshape(batch, seq_len, d_model)
        return out @ out_w.T + out_b

    def _L0_attn_b_ref(x, Wq_down, Wk_down, Wv_down, Wq_up_c, Wq_up_e, Wk_up_c, Wk_up_e, Wv_up, Wc):
        import jax, jax.numpy as jnp
        import numpy as np
        import math
        B, T, C = (2, 256, 128)
        H, L = (16, 64)
        DH = C // H
        DHE = DH // 2
        THETA = 10000.0

        def _rope_cache(t, dim):
            inv_freq = 1.0 / THETA ** (jnp.arange(0, dim, 2, dtype=jnp.float32) / dim)
            freqs = jnp.arange(t, dtype=jnp.float32)[:, None] * inv_freq[None, :]
            emb = jnp.concatenate((freqs, freqs), axis=-1)
            return (jnp.cos(emb), jnp.sin(emb))

        def _apply_rope(x, cos, sin):
            x1 = x[..., 0::2]
            x2 = x[..., 1::2]
            rot = jnp.stack((-x2, x1), axis=-1).reshape(x.shape)
            return x * cos[None, None] + rot * sin[None, None]
        b, t, c = x.shape
        q_lat = (x @ Wq_down).reshape(b, t, H, L)
        k_lat = (x @ Wk_down).reshape(b, t, H, L)
        v_lat = (x @ Wv_down).reshape(b, t, H, L)
        q_c = jnp.einsum('bthl,ld->bhtd', q_lat, Wq_up_c)
        q_e = jnp.einsum('bthl,ld->bhtd', q_lat, Wq_up_e)
        k_c = jnp.einsum('bthl,ld->bhtd', k_lat, Wk_up_c)
        k_e = jnp.einsum('bthl,ld->bhtd', k_lat, Wk_up_e)
        v = jnp.einsum('bthl,ld->bhtd', v_lat, Wv_up)
        cos, sin = _rope_cache(t, DHE)
        q = jnp.concatenate([q_c, _apply_rope(q_e, cos, sin)], axis=-1)
        k = jnp.concatenate([k_c, _apply_rope(k_e, cos, sin)], axis=-1)
        scale = 1.0 / math.sqrt(DH)
        scores = jnp.einsum('bhqd,bhkd->bhqk', q, k) * scale
        causal = jnp.tril(jnp.ones((t, t), dtype=bool))
        scores = jnp.where(causal[None, None], scores, -jnp.inf)
        att = jax.nn.softmax(scores, axis=-1)
        y = jnp.einsum('bhqk,bhkd->bhqd', att, v)
        y = y.transpose(0, 2, 1, 3).reshape(b, t, c)
        return y @ Wc

    def _L0_ffn_ref(x, W_exp, b_exp, up_weights, up_bias, down_weights, W_con, b_con, down_bias):
        import jax, jax.numpy as jnp
        import numpy as np
        D_MODEL = 128
        EXPANSION = 4
        D_HIDDEN = D_MODEL * EXPANSION
        NUM_STAGES = int(np.log2(D_HIDDEN))

        def butterfly(y, weights, dim):
            lead = y.shape[:-1]
            for stage in range(weights.shape[0]):
                s = 2 ** stage
                nb = dim // (2 * s)
                yr = y.reshape(*lead, nb, 2, s)
                a = yr[..., 0, :]
                b = yr[..., 1, :]
                w = weights[stage].reshape(nb, s, 2, 2)
                na = w[..., 0, 0] * a + w[..., 0, 1] * b
                nb2 = w[..., 1, 0] * a + w[..., 1, 1] * b
                y = jnp.stack([na, nb2], axis=-2).reshape(*lead, dim)
            return y
        h = jnp.einsum('bsd,dh->bsh', x, W_exp) + b_exp
        h = butterfly(h, up_weights, D_HIDDEN)
        h = jax.nn.gelu(h + up_bias, approximate=False)
        h = butterfly(h, down_weights, D_HIDDEN)
        y = jnp.einsum('bsh,hd->bsd', h, W_con) + b_con
        return y + down_bias
    x = L0_attn_a_x
    x = x + _L0_attn_a_ref(_layernorm(x, axis=-1), L0_attn_a_qkv_w, L0_attn_a_qkv_b, L0_attn_a_out_w, L0_attn_a_out_b)
    x = x + _L0_ffn_ref(_layernorm(x, axis=-1), L0_ffn_W_exp, L0_ffn_b_exp, L0_ffn_up_weights, L0_ffn_up_bias, L0_ffn_down_weights, L0_ffn_W_con, L0_ffn_b_con, L0_ffn_down_bias)
    x = x + _L0_attn_b_ref(_layernorm(x, axis=-1), L0_attn_b_Wq_down, L0_attn_b_Wk_down, L0_attn_b_Wv_down, L0_attn_b_Wq_up_c, L0_attn_b_Wq_up_e, L0_attn_b_Wk_up_c, L0_attn_b_Wk_up_e, L0_attn_b_Wv_up, L0_attn_b_Wc)
    x = x + _L0_ffn_ref(_layernorm(x, axis=-1), L0_ffn_W_exp, L0_ffn_b_exp, L0_ffn_up_weights, L0_ffn_up_bias, L0_ffn_down_weights, L0_ffn_W_con, L0_ffn_b_con, L0_ffn_down_bias)
    return x

_drawn_inputs = setup_inputs


def setup_inputs(seed=0):
    import zlib

    import numpy as np

    out = dict(_drawn_inputs(seed))
    spreads = {'L0_attn_a_qkv_b': (0.0, 0.1),
     'L0_attn_a_out_b': (0.0, 0.1),
     'L0_ffn_b_exp': (0.0, 0.1),
     'L0_ffn_up_bias': (0.0, 0.1),
     'L0_ffn_b_con': (0.0, 0.1),
     'L0_ffn_down_bias': (0.0, 0.1)}
    factors = {'L0_attn_b_Wq_down': 8.0,
     'L0_attn_b_Wk_down': 8.0,
     'L0_attn_b_Wv_down': 8.0,
     'L0_attn_b_Wq_up_c': 8.0,
     'L0_attn_b_Wq_up_e': 8.0,
     'L0_attn_b_Wk_up_c': 8.0,
     'L0_attn_b_Wk_up_e': 8.0,
     'L0_attn_b_Wv_up': 8.0,
     'L0_attn_b_Wc': 8.0}
    for name, (base, spread) in spreads.items():
        noise = np.random.default_rng([zlib.crc32(name.encode()), seed]).standard_normal(out[name].shape)
        drawn = base * np.exp(spread * noise) if base else spread * noise
        out[name] = jnp.asarray(drawn.astype(out[name].dtype))
    for name, factor in factors.items():
        out[name] = (out[name] * factor).astype(out[name].dtype)
    return out
```

```python
from contextlib import ExitStack

import numpy as np

import concourse.bass as bass
from concourse import mybir

P = 128
B = 4
T = 1024
D = 128
H = 16
DH = D // H
HG = 4
G = H // HG
KT = T // P
CH = 512
CT = CH // P
NC = T // CH
HID = 512
HC = HID // P
STAGES = 9
LAT = 64
VW = DH + 1
SPLIT = 3
R_SPLIT = SPLIT * SPLIT * DH
R_BIAS = 3 * KT
R_MAX = R_SPLIT + R_BIAS
R_ALL = R_MAX + SPLIT
LEAD = 4
EPS = 1e-5
SCALE = float(np.float32(1.0) / np.sqrt(np.float32(DH)))
BIG = 1e30

F32 = mybir.dt.float32
BF16 = mybir.dt.bfloat16
ALU = mybir.AluOpType
ACT = mybir.ActivationFunctionType
AX_X = mybir.AxisListType.X


def attention_plan(causal):
    steps, pieces = [], []
    for qc in range(NC):
        for kb in range(KT):
            lo = max(0, kb * P - qc * CH) if causal else 0
            if lo < CH:
                steps.append((qc, kb, lo))
    for h in range(HG):
        for qt in range(KT):
            for half in range(NC):
                width = min(CH, (qt + 1) * P - half * CH) if causal else CH
                if width > 0:
                    at = qt * P - half * CH
                    pieces.append((h, qt, half, width, at if 0 <= at < width else None))
    return steps, pieces


def build(nc, x, out, wqkv, bqk, bv, wout_a, bout, ident, identb, alibi_q, alibi_k, dist, mask,
          down_t, up, sign, cos, sin, wout_b, w_exp, b_exp, up_w, up_bias, down_w, w_con_t, b_con,
          down_bias):
    ctx = ExitStack()
    with ctx:
        def sb(name, shape, dt=F32):
            return ctx.enter_context(nc.sbuf_tensor(name, shape, dt))

        def sem(name):
            return ctx.enter_context(nc.semaphore(name))

        def sems(name, n):
            return [sem(f"{name}{i}") for i in range(n)]

        def dram(name, shape, dt):
            return nc.dram_tensor(name, shape, dt, kind="Internal").ap()

        X = sb("X", [P, B * KT, D])
        O = sb("O", [P, B * KT, D])
        V = sb("V", [P, B, KT, H * VW])
        QA = sb("QA", [R_ALL, G, HG, T], BF16)
        KA = sb("KA", [R_ALL, G, HG, T], BF16)
        VR = sb("VR", [P, G, KT, HG * VW])
        DIST = sb("DIST", [P, H, P], BF16)
        MASK = sb("MASK", [P, 2, P], BF16)
        IDB = sb("IDB", [P, P], BF16)
        ID = sb("ID", [P, P])
        MX = sb("MX", [P, 2, HG * KT, NC])
        NM = sb("NM", [P, 3, HG * KT])
        MP = sb("MP", [P, 2, SPLIT, HG * KT], BF16)
        MT = sb("MT", [SPLIT * HG * KT, G, P], BF16)
        OT = sb("OT", [P, NC, CH])
        RD = sb("RD", [P, 2, CT * HG])
        WQKV = sb("WQKV", [P, 3, D])
        BQK = sb("BQK", [P, 2])
        BV = sb("BV", [P, D])
        WOUT = sb("WOUT", [P, 2, D])
        BOUT = sb("BOUT", [P, D])
        WB = sb("WB", [P, 5, D])
        UP = sb("UP", [P, 5, DH])
        SIGN = sb("SIGN", [P, DH])
        BD = sb("BD", [P, 5, 2, DH])
        COS = sb("COS", [P, T])
        SIN = sb("SIN", [P, T])
        WUP = sb("WUP", [P, HID])
        BUP = sb("BUP", [P, HC])
        UPB = sb("UPB", [P, HC])
        WDNT = sb("WDNT", [P, HID])
        WDN = sb("WDN", [P, HC, D])
        BEFF = sb("BEFF", [1, HID])
        FB = sb("FB", [P, 2, D])
        HALF = sb("HALF", [P, CT])
        CHAIN = 10 * CH
        WORK = sb("WORK", [P, 2 * CHAIN])
        SPL = sb("SPL", [P, 2, 2, SPLIT, CH], BF16)
        STATS = sb("STATS", [P, 2, CT, 6])
        MV = sb("MV", [P, 2, CT, 2])
        VE = sb("VE", [P, 2, CT])
        RS = sb("RS", [P, 2, CT])

        def work(j, at, n=1):
            return WORK[:, j * CHAIN + at * CH:j * CHAIN + (at + n) * CH]

        xn = [work(j, 0) for j in range(2)]
        xt = [work(j, 1) for j in range(2)]
        os_ = [work(j, 2) for j in range(2)]
        ott = [work(j, 3) for j in range(2)]
        gel = [work(j, 4, HC) for j in range(2)]
        q32 = [work(j, 8) for j in range(2)]
        rot = [work(j, 9) for j in range(2)]
        rest = xn
        PR = WORK[:, 0:4 * 2 * CH].rearrange("p (s h q) -> p s h q", s=4, h=2)
        DOWN = WORK[:, 0:3 * 8 * P].rearrange("p (k j c) -> p k j c", k=3, j=8)
        at = 8 * CH
        WST = WORK[:, at:at + 4 * CH].rearrange("p (b w) -> p b w", b=2)
        TMP = WORK[:, at + 4 * CH:at + 6 * CH].rearrange("p (b w) -> p b w", b=4)
        YW = WORK[:, at + 6 * CH:at + 8 * CH].rearrange("p (b w) -> p b w", b=2)
        YB = WORK[:, at + 8 * CH:at + 10 * CH].rearrange("p (b w) -> p b w", b=2)
        YC = WORK[:, at + 10 * CH:at + 12 * CH].rearrange("p (b w) -> p b w", b=2)

        PS = ctx.enter_context(nc.psum_tensor("PS", [P, 8, CH], F32))
        SM_BANK, OT_BANK = 4, 6

        qs = [dram(f"qs{i}", [B, SPLIT, DH, H, T], BF16) for i in range(2)]
        ks = [dram(f"ks{i}", [B, SPLIT, DH, H, T], BF16) for i in range(2)]

        x_in = sem("x_in")
        consts_in = sem("consts_in")
        bias_rows_in = sem("bias_rows_in")
        phase = sem("phase")
        setup = sem("setup")
        apart = sem("apart")
        fold = sem("fold")
        folded = sem("folded")
        folded_pe = sem("folded_pe")
        bfly_in = sems("bfly_in", 2)
        bfly = sem("bfly")
        out_sem = sem("out_sem")

        block = ctx.enter_context(nc.Block())
        ENGINES = 5
        X_LOADS = B + 4

        def wait_apart(e, s, value):
            e.wait_ge(s, value)
            e.sem_inc(apart, 1)

        def end_phase(e, n):
            e.drain().then_inc(phase, 1)
            e.wait_ge(phase, ENGINES * n)

        class Chunks:

            def __init__(self, name, layer, attended, ffn, project):
                self.layer, self.attended, self.ffn, self.project = layer, attended, ffn, project
                self.norms = 1 + (1 if attended and project is not None else 0)
                self.turns = self.norms + (1 if attended else 0)
                self.wides = (HC if ffn else 0) + (0 if project is None else (2 if project == 0 else 4))
                self.rows = (1 if attended else 0) + (1 if ffn else 0) + (0 if project is None else 1)
                self.split = 4 if project == 0 else 5
                self.o_copied = sems(f"{name}_o_copied", 2)
                self.x_biased = sems(f"{name}_x_biased", 2)
                self.x_added = sems(f"{name}_x_added", 2)
                self.stats_done = sems(f"{name}_stats_done", 2)
                self.mv_done = sems(f"{name}_mv_done", 2)
                self.var_ready = sems(f"{name}_var_ready", 2)
                self.rstd_ready = sems(f"{name}_rstd_ready", 2)
                self.xn_ready = sems(f"{name}_xn_ready", 2)
                self.turn_full = sems(f"{name}_turn_full", 2)
                self.turn_free = sems(f"{name}_turn_free", 2)
                self.row_full = sems(f"{name}_row_full", 2)
                self.row_free = sems(f"{name}_row_free", 2)
                self.wide_full = sems(f"{name}_wide_full", 2)
                self.wide_free = sems(f"{name}_wide_free", 2)
                self.split_step = sems(f"{name}_split_step", 2)
                self.stored = sems(f"{name}_stored", 2)

        CA = Chunks("pa", 0, False, False, 0)
        CB = Chunks("pb", 0, True, True, 1)
        CC = Chunks("pc", 1, True, True, None)

        def bank(j, i):
            return PS[:, 4 * j + i, :]

        def tile0(it, j):
            return it * KT + j * CT

        def chunks_pe(pe, c):
            def turn(it, j, i, src):
                pe.wait_ge(c.turn_free[j], it * c.turns + (i + 1))
                for t in range(CT):
                    mm = pe.transpose(bank(j, 0)[:, t * P:(t + 1) * P], src[:, t * P:(t + 1) * P], ID[:, :])
                mm.then_inc(c.turn_full[j], 1)

            def normed(it, j, i, k):
                pe.wait_ge(c.xn_ready[j], it * c.norms + (k + 1))
                turn(it, j, i, xn[j])

            def wide(it, j, n, lhs):
                pe.wait_ge(c.wide_free[j], it * c.wides + (n + 1))
                pe.matmul(bank(j, 2 + n % 2), lhs, xt[j], start=True, stop=True).then_inc(c.wide_full[j], 1)

            def row_bank(it, j, n):
                pe.wait_ge(c.row_free[j], it * c.rows + (n + 1))

            for j in range(2):
                pe.sem_inc(c.row_full[j], 1)
            with pe.Fori(0, B) as it:
                turns = 0
                if c.attended:
                    for j in range(2):
                        pe.wait_ge(c.o_copied[j], it + 1)
                        turn(it, j, 0, os_[j])
                    for j in range(2):
                        pe.wait_ge(c.turn_free[j], it * c.turns + 2)
                        row_bank(it, j, 0)
                        for t in range(CT):
                            mm = pe.matmul(bank(j, 1)[:, t * P:(t + 1) * P], ott[j][:, t * P:(t + 1) * P],
                                           WOUT[:, c.layer, :], start=True, stop=True)
                        mm.then_inc(c.row_full[j], 1)
                    turns = 1
                for j in range(2):
                    normed(it, j, turns, 0)
                for j in range(2):
                    pe.wait_ge(c.turn_free[j], it * c.turns + (turns + 2))
                turns += 1
                if c.ffn:
                    for n in range(HC):
                        for j in range(2):
                            wide(it, j, n, WUP[:, n * P:(n + 1) * P])
                    for j in range(2):
                        row_bank(it, j, 1)
                        pe.wait_ge(c.wide_free[j], it * c.wides + (HC + 2))
                        for t in range(CT):
                            for n in range(HC):
                                mm = pe.matmul(bank(j, 1)[:, t * P:(t + 1) * P],
                                               gel[j][:, n * CH + t * P:n * CH + (t + 1) * P],
                                               WDN[:, n, :], start=(n == 0), stop=(n == HC - 1))
                        mm.then_inc(c.row_full[j], 1)
                    if c.project is not None:
                        for j in range(2):
                            normed(it, j, turns, 1)
                        for j in range(2):
                            pe.wait_ge(c.turn_free[j], it * c.turns + (turns + 2))
                if c.project is not None:
                    first = HC if c.ffn else 0
                    for j in range(2):
                        for k in range(c.wides - first):
                            wide(it, j, first + k, WQKV[:, k, :] if c.project == 0 else WB[:, k, :])
                    for j in range(2):
                        row_bank(it, j, c.rows - 1)
                        for t in range(CT):
                            mm = pe.matmul(bank(j, 1)[:, t * P:(t + 1) * P], xt[j][:, t * P:(t + 1) * P],
                                           WQKV[:, 2, :] if c.project == 0 else WB[:, 4, :],
                                           start=True, stop=True)
                        mm.then_inc(c.row_full[j], 1)

        def chunks_act(act, c):
            def turn(it, j, i, dst):
                act.wait_ge(c.turn_full[j], it * c.turns + (i + 1))
                act.wait_ge(c.row_full[j], it * c.rows + 1)
                nc.scalar.copy(dst, bank(j, 0)).then_inc(c.turn_free[j], 1)

            for j in range(2):
                act.sem_inc(c.turn_free[j], 1)
                act.sem_inc(c.wide_free[j], 2)
            with act.Fori(0, B) as it:
                turns = 0
                if c.attended:
                    for j in range(2):
                        turn(it, j, 0, ott[j])
                    turns = 1
                for j in range(2):
                    turn(it, j, turns, xt[j])
                if c.ffn:
                    for n in range(HC):
                        for j in range(2):
                            act.wait_ge(c.wide_full[j], it * c.wides + (n + 1))
                            if n == 0:
                                act.wait_ge(c.row_full[j], it * c.rows + 2)
                            nc.scalar.activation(gel[j][:, n * CH:(n + 1) * CH], bank(j, 2 + n % 2), ACT.Gelu,
                                                 bias=BUP[:, n:n + 1]).then_inc(c.wide_free[j], 1)
                    if c.project is not None:
                        for j in range(2):
                            turn(it, j, turns + 1, xt[j])

        def chunks_pool(pool, c):
            with pool.Fori(0, B) as it:
                if c.attended:
                    for j in range(2):
                        wait_apart(pool, c.turn_free[j], it * c.turns + 1)
                        nc.gpsimd.tensor_copy(os_[j].rearrange("p (t d) -> p t d", t=CT),
                                              O[:, bass.ds(tile0(it, j), CT), :]).then_inc(c.o_copied[j], 1)
                        if c.layer == 0:
                            xs = X[:, bass.ds(tile0(it, j), CT), :]
                            nc.gpsimd.tensor_tensor(xs, xs, BOUT[:, :].unsqueeze(1).broadcast_to([P, CT, D]),
                                                    ALU.add).then_inc(c.x_biased[j], 1)
                for k in range(c.norms):
                    for j in range(2):
                        pool.wait_ge(c.var_ready[j], it * c.norms + (k + 1))
                        nc.gpsimd.tensor_tensor(RS[:, j, :], VE[:, j, :], HALF[:, :],
                                                ALU.pow).then_inc(c.rstd_ready[j], 1)

        def chunks_dve(dve, c):
            def xs(it, j):
                return X[:, bass.ds(tile0(it, j), CT), :]

            def four(ap):
                return ap.rearrange("p (t d) -> p t d", t=CT)

            def add(it, j, n, k):
                dve.wait_ge(c.row_full[j], it * c.rows + (n + 2))
                if n == 0 and c.layer == 0:
                    dve.wait_ge(c.x_biased[j], it + 1)
                nc.vector.tensor_tensor(xs(it, j), four(bank(j, 1)), xs(it, j), ALU.add).then_inc(c.x_added[j], 1)
                dve.wait_ge(c.x_added[j], it * adds + (k + 1))

            def free_row(j):
                dve.sem_inc(c.row_free[j], 1)

            adds = (1 if c.attended else 0) + (2 if c.ffn else 0)

            def stats(it, j, k):
                for t in range(CT):
                    s = nc.vector.bn_stats(STATS[:, j, t, :],
                                           X[:, bass.ds(tile0(it, j) + t, 1), :].rearrange("p a d -> p (a d)"))
                s.then_inc(c.stats_done[j], 1)
                wait_apart(dve, c.stats_done[j], it * c.norms + (k + 1))
                for t in range(CT):
                    s = nc.vector.bn_aggr(MV[:, j, t, :], STATS[:, j, t, :])
                s.then_inc(c.mv_done[j], 1)
                dve.wait_ge(c.mv_done[j], it * c.norms + (k + 1))
                nc.vector.tensor_scalar(VE[:, j, :], MV[:, j, :, 1], EPS, None, ALU.add).then_inc(c.var_ready[j], 1)

            def norm(it, j, i, k):
                dve.wait_ge(c.rstd_ready[j], it * c.norms + (k + 1))
                dve.wait_ge(c.turn_free[j], it * c.turns + (i + 1))
                for t in range(CT):
                    s = nc.vector.tensor_scalar(xn[j][:, t * P:(t + 1) * P],
                                                X[:, bass.ds(tile0(it, j) + t, 1), :].rearrange("p a d -> p (a d)"),
                                                MV[:, j, t, 0:1], RS[:, j, t:t + 1], ALU.subtract, ALU.mult)
                s.then_inc(c.xn_ready[j], 1)

            def ffn_bias(it, j, k):
                dve.wait_ge(c.xn_ready[j], it * c.norms + 1)
                nc.vector.tensor_tensor(xs(it, j), xs(it, j),
                                        FB[:, 0, :].unsqueeze(1).broadcast_to([P, CT, D]), ALU.add)\
                    .then_inc(c.x_added[j], 1)
                dve.wait_ge(c.x_added[j], it * adds + (k + 1))

            def project(it, j, first):
                step = it * 2 * c.split
                dve.wait_ge(c.stored[j], it * 32 + 1)
                for qk in range(2):
                    scale = SCALE if qk == 0 else 1.0
                    s0 = qk * c.split
                    if c.project == 0:
                        n = first + qk
                        dve.wait_ge(c.wide_full[j], it * c.wides + (n + 1))
                        nc.vector.tensor_scalar(q32[j], bank(j, 2 + n % 2), BQK[:, qk:qk + 1], scale,
                                                ALU.add, ALU.mult).then_inc(c.wide_free[j], 1)
                        dve.wait_ge(c.wide_free[j], it * c.wides + (n + 3))
                    else:
                        cols = slice(j * CH, (j + 1) * CH)
                        for i, (dst, table) in enumerate(((rest[j], COS), (rot[j], SIN))):
                            n = first + 2 * qk + i
                            dve.wait_ge(c.wide_full[j], it * c.wides + (n + 1))
                            nc.vector.scalar_tensor_tensor(out=dst, in0=bank(j, 2 + n % 2), scalar=scale,
                                                           in1=table[:, cols], op0=ALU.mult,
                                                           op1=ALU.mult).then_inc(c.wide_free[j], 1)
                        dve.wait_ge(c.wide_free[j], it * c.wides + (n + 3))
                        nc.vector.tensor_tensor(q32[j], rest[j], rot[j], ALU.add).then_inc(c.split_step[j], 1)
                        s0 += 1
                        dve.wait_ge(c.split_step[j], step + s0)
                    for k, (dst, a, b) in enumerate(((SPL[:, j, qk, 0, :], q32[j], None),
                                                     (rest[j], q32[j], SPL[:, j, qk, 0, :]),
                                                     (SPL[:, j, qk, 1, :], rest[j], None),
                                                     (SPL[:, j, qk, 2, :], rest[j], SPL[:, j, qk, 1, :]))):
                        if b is None:
                            s = nc.vector.tensor_copy(dst, a)
                        else:
                            s = nc.vector.tensor_tensor(dst, a, b, ALU.subtract)
                        s.then_inc(c.split_step[j], 1)
                        s0 += 1
                        dve.wait_ge(c.split_step[j], step + s0)

            def values(it, j):
                n = c.rows - 1
                dve.wait_ge(c.row_full[j], it * c.rows + (n + 2))
                for t in range(CT):
                    dst = V[:, bass.ds(it, 1), j * CT + t, :].rearrange("p a (h w) -> p (a h) w", h=H)[:, :, 0:DH]
                    src = bank(j, 1)[:, t * P:(t + 1) * P].rearrange("p (h d) -> p h d", h=H)
                    if c.project == 0:
                        s = nc.vector.tensor_tensor(dst, src, BV[:, :].rearrange("p (h d) -> p h d", h=H), ALU.add)
                    else:
                        s = nc.vector.tensor_copy(dst, src)
                s.then_inc(c.row_free[j], 1)

            for j in range(2):
                dve.sem_inc(c.row_free[j], 1)
            with dve.Fori(0, B) as it:
                turns, k = 0, 0
                if c.attended:
                    for j in range(2):
                        add(it, j, 0, 0)
                        free_row(j)
                        stats(it, j, 0)
                    turns, k = 1, 1
                else:
                    for j in range(2):
                        stats(it, j, 0)
                for j in range(2):
                    norm(it, j, turns, 0)
                if c.ffn:
                    for j in range(2):
                        ffn_bias(it, j, 1)
                        add(it, j, 1, 2)
                        free_row(j)
                        if c.project is not None:
                            stats(it, j, 1)
                    if c.project is not None:
                        for j in range(2):
                            norm(it, j, turns + 1, 1)
                if c.project is not None:
                    for j in range(2):
                        project(it, j, HC if c.ffn else 0)
                    for j in range(2):
                        values(it, j)

        def chunks_sp(sp, c):
            if c.project is not None:
                for j in range(2):
                    sp.sem_inc(c.stored[j], 1)
            with sp.Fori(0, B) as it:
                for j in range(2):
                    if c.project is None:
                        sp.wait_ge(c.x_added[j], it * 3 + 3)
                        sp.dma_start(out[bass.ds(it, 1), j * CH:(j + 1) * CH, :]
                                     .rearrange("a (t p) d -> p (a t) d", p=P),
                                     X[:, bass.ds(tile0(it, j), CT), :]).then_inc(out_sem, 16)
                        continue
                    for qk, scratch in enumerate((qs[c.project], ks[c.project])):
                        sp.wait_ge(c.split_step[j], it * 2 * c.split + (qk + 1) * c.split)
                        sp.dma_start(scratch[bass.ds(it, 1), :, :, :, j * CH:(j + 1) * CH]
                                     .rearrange("a s d h t -> (d h) (a s) t"),
                                     SPL[:, j, qk, :, :]).then_inc(c.stored[j], 16)
            for j in range(2):
                if c.project is not None:
                    sp.wait_ge(c.stored[j], 32 * B + 1)
            if c.project is None:
                sp.wait_ge(out_sem, 16 * 2 * B)

        class Attention:
            def __init__(self, layer):
                self.layer = layer
                self.steps, self.pieces = attention_plan(layer == 1)
                self.ns = len(self.steps)
                self.per = len(self.pieces) // self.ns
                assert self.per * self.ns == len(self.pieces)
                n = "ab"[layer]
                self.loaded = sems(f"{n}_loaded", G)
                self.maxed = sems(f"{n}_maxed", G)
                self.values = sem(f"{n}_values")
                self.st_full = sem(f"{n}_st_full")
                self.exp_done = sem(f"{n}_exp_done")
                self.pv_done = sem(f"{n}_pv_done")
                self.ot_free = sem(f"{n}_ot_free")
                self.ot_turned = sem(f"{n}_ot_turned")
                self.sm_full = sem(f"{n}_sm_full")
                self.sm_free = sem(f"{n}_sm_free")
                self.parts = sem(f"{n}_parts")
                self.dchain = sem(f"{n}_dchain")
                self.before = [("piece", 0, i) for i in range(len(self.pieces))] + [("rows", 0)]
                self.before += [("piece", 1, i) for i in range(LEAD * self.per)]
                self.base = len(self.before)
                self.order = {}
                n = 0
                for g in range(G):
                    for s in range(self.ns):
                        self.order[g, s] = (n, self.items(g, s))
                        n += len(self.order[g, s][1])
                self.total = n
                assert n % 2 == 0

            def items(self, g, s):
                ns, per = self.ns, self.per
                p = g * ns + s + LEAD
                items = [("piece", p // ns + 1, (p % ns) * per + i) for i in range(per)]
                if s == ns - LEAD + 1:
                    items.append(("rows", g + 1))
                half = next(i for i, (qc, _, _) in enumerate(self.steps) if qc == 1)
                if s == half + 3:
                    items.append(("out", g, 0))
                if g and s == 2:
                    items.append(("out", g - 1, 1))
                if g == G - 1 and s == ns - 1:
                    items.append(("out", g, 1))
                return items

            def side(self, it, last, g, s):
                n, items = self.order[g, s]
                if not last:
                    return [(it * self.total + (self.base + n + i), (self.base + n + i) % 2, x)
                            for i, x in enumerate(items)]
                n = it * self.total + self.base
                result = []
                for gg in range(G):
                    for ss in range(self.ns):
                        for x in self.order[gg, ss][1]:
                            if x[0] != "out" and x[1] >= G:
                                continue
                            if (gg, ss) == (g, s):
                                result.append((n, n % 2, x))
                            n += 1
                return result

        AA, AB = Attention(0), Attention(1)

        def batches(e, body):
            with e.Fori(0, B - 1) as it:
                body(it, False)
            body(B - 1, True)

        def unit_of(it, g):
            return (it, g) if g < G else (it + 1, g - G)

        def attention_pe(pe, a):
            ns = a.ns

            def scores(it, g, s, pair, m):
                b, g = unit_of(it, g)
                qc, kb, lo = a.steps[s]
                if s == 0 and pair == 0:
                    pe.wait_ge(a.maxed[g], (b + 1) * 48)
                if m is not None:
                    pe.wait_ge(a.exp_done, m)
                for hh in range(2):
                    h = 2 * pair + hh
                    diagonal = kb * P - qc * CH
                    has = 0 <= diagonal < CH
                    mm = pe.matmul(PS[:, 2 * pair + hh, lo:CH], KA[:, g, h, kb * P:(kb + 1) * P],
                                   QA[:, g, h, qc * CH + lo:(qc + 1) * CH], start=True, stop=not has)
                    if has:
                        block = DIST[:, g * HG + h, :] if a.layer == 0 else MASK[:, 0, :]
                        mm = pe.matmul(PS[:, 2 * pair + hh, diagonal:diagonal + P], IDB[:, :], block,
                                       start=False, stop=True)
                mm.then_inc(a.st_full, 1)

            def weighted(it, g, s):
                qc, kb, lo = a.steps[s]
                t = it * (G * ns) + (g * ns + s)
                if s == 0:
                    pe.wait_ge(a.values, it * G + (g + 1))
                if kb == 0:
                    pe.wait_ge(a.ot_free, it * (G * NC) + (NC * g + qc + 1))
                pe.wait_ge(a.exp_done, t * 2 + 2)
                last = s + 1 == ns or a.steps[s + 1][0] != qc
                for h in range(HG):
                    mm = pe.matmul(PS[32 * h:32 * h + VW, OT_BANK + qc, lo:CH],
                                   VR[:, g, kb, h * VW:(h + 1) * VW],
                                   PR[:, 2 * ((g * ns + s) % 2) + h // 2, h % 2, lo:CH],
                                   start=(kb == 0), stop=last)
                mm.then_inc(a.pv_done, 1)

            def side(it, n, slot, item, first):
                kind = item[0]
                if not first:
                    pe.wait_ge(a.sm_free, n - 1)
                bank_ = PS[:, SM_BANK + slot, :]
                if kind == "piece":
                    b, g = unit_of(it, item[1])
                    h, qt, half, width, diagonal = a.pieces[item[2]]
                    if item[2] == 0:
                        pe.wait_ge(a.loaded[g], (b + 1) * 16 * SPLIT * (SPLIT + 1))
                    mm = pe.matmul(bank_[:, 0:width], QA[0:R_MAX, g, h, qt * P:(qt + 1) * P],
                                   KA[0:R_MAX, g, h, half * CH:half * CH + width],
                                   start=True, stop=diagonal is None)
                    if diagonal is not None:
                        block = DIST[:, g * HG + h, :] if a.layer == 0 else MASK[:, 1, :]
                        mm = pe.matmul(bank_[:, diagonal:diagonal + P], IDB[:, :], block, start=False, stop=True)
                elif kind == "rows":
                    pe.wait_ge(a.parts, it * G + (item[1] + 1))
                    mm = pe.transpose(bank_.bitcast(BF16)[0:SPLIT * HG * KT, 0:P],
                                      MP[:, item[1] % 2, :, :].rearrange("p s r -> p (s r)"), IDB[:, :])
                else:
                    o = NC * item[1] + item[2]
                    pe.wait_ge(a.ot_free, it * (G * NC) + (o + 3))
                    for t in range(CT):
                        mm = pe.transpose(bank_[:, t * P:(t + 1) * P], OT[:, item[2], t * P:(t + 1) * P], ID[:, :])
                mm.then_inc(a.sm_full, 1)

            pe.sem_inc(a.pv_done, 1)
            for n, item in enumerate(a.before):
                side(0, n, n % 2, item, n < 2)
            for pair in range(2):
                scores(0, 0, 0, pair, None)

            def body(it, last):
                for g in range(G):
                    for s in range(ns):
                        todo = a.side(it, last, g, s)
                        if g == G - 1 and s == ns - 1:
                            todo, tail = todo[:-1], todo[-1:]
                        else:
                            tail = []
                        cut = [todo[:2], todo[2:]]
                        following = (g, s + 1) if s + 1 < ns else (g + 1, 0)
                        t = it * (G * ns) + (g * ns + s)
                        for pair in range(2):
                            if not (last and following[0] == G):
                                scores(it, following[0], following[1], pair, t * 2 + (pair + 1))
                            if pair:
                                weighted(it, g, s)
                            for n, slot, item in cut[pair]:
                                side(it, n, slot, item, False)
                        for n, slot, item in tail:
                            side(it, n, slot, item, False)

            batches(pe, body)

        def attention_act(act, a):
            ns = a.ns

            def exps(it, g, s, pair, first=False):
                lo = a.steps[s][2]
                t = it * (G * ns) + (g * ns + s)
                act.wait_ge(a.st_full, t * 2 + (pair + 1))
                if not first:
                    act.wait_ge(a.pv_done, t)
                nc.scalar.activation(PR[:, 2 * ((g * ns + s) % 2) + pair, :, lo:CH],
                                     PS[:, 2 * pair:2 * pair + 2, lo:CH], ACT.Exp).then_inc(a.exp_done, 1)

            act.sem_inc(a.ot_free, 2)
            for pair in range(2):
                exps(0, 0, 0, pair, True)

            def body(it, last):
                for g in range(G):
                    for s in range(ns):
                        qc = a.steps[s][0]
                        for pair in range(2):
                            f = (g, s + 1) if s + 1 < ns else (g + 1, 0)
                            if not (last and f[0] == G):
                                exps(it, f[0], f[1], pair)
                        if s + 1 == ns or a.steps[s + 1][0] != qc:
                            t = it * (G * ns) + (g * ns + s)
                            act.wait_ge(a.pv_done, t + 2)
                            act.wait_ge(a.ot_turned, it * (G * NC) + (NC * g + qc + 1))
                            nc.scalar.copy(OT[:, qc, :], PS[:, OT_BANK + qc, :]).then_inc(a.ot_free, 1)

            batches(act, body)

        def attention_dve(dve, a):
            RCHAIN = 5

            def split_max(it, g):
                v = it * G + g
                b2 = g % 2
                mx, mp = MX[:, b2, :, :], MP[:, b2, :, :]
                ops = [lambda: nc.vector.tensor_reduce(NM[:, 0, :], mx, AX_X, ALU.max, negate=True),
                       lambda: nc.vector.tensor_copy(mp[:, 0, :], NM[:, 0, :]),
                       lambda: nc.vector.tensor_tensor(NM[:, 1, :], NM[:, 0, :], mp[:, 0, :], ALU.subtract),
                       lambda: nc.vector.tensor_copy(mp[:, 1, :], NM[:, 1, :])]
                for k, op in enumerate(ops):
                    dve.wait_ge(a.dchain, v * RCHAIN + (k + 1))
                    op().then_inc(a.dchain, 1)
                dve.wait_ge(a.dchain, v * RCHAIN + 5)
                nc.vector.tensor_tensor(mp[:, 2, :], NM[:, 1, :], mp[:, 1, :], ALU.subtract).then_inc(a.parts, 1)

            def side(it, n, slot, item):
                kind = item[0]
                dve.wait_ge(a.sm_full, n + 1)
                bank_ = PS[:, SM_BANK + slot, :]
                if kind == "piece":
                    h, qt, half, width, _ = a.pieces[item[2]]
                    last = item[2] == len(a.pieces) - 1
                    nc.vector.tensor_reduce(MX[:, item[1] % 2, h * KT + qt, half:half + 1], bank_[:, 0:width],
                                            AX_X, ALU.max).then_inc(a.sm_free, 1)
                    if last:
                        dve.wait_ge(a.sm_free, n + 1)
                        dve.sem_inc(a.dchain, 1)
                        split_max(it, item[1])
                elif kind == "rows":
                    nc.vector.tensor_copy(MT[:, item[1] % G, :],
                                          bank_.bitcast(BF16)[0:SPLIT * HG * KT, 0:P]).then_inc(a.sm_free, 1)
                else:
                    g, qc = item[1], item[2]
                    o = NC * g + qc
                    rows = bank_.rearrange("p (t h r) -> p t h r", t=CT, h=HG)
                    rd = RD[:, qc, :].rearrange("p (t h) -> p t h", t=CT)
                    nc.vector.reciprocal(rd, rows[:, :, :, DH]).then_inc(a.ot_turned, 1)
                    dve.wait_ge(a.ot_turned, it * (G * NC) + (o + 3))
                    dst = O[:, bass.ds(it * KT + qc * CT, CT), g * HG * DH:(g + 1) * HG * DH]
                    nc.vector.tensor_tensor(dst.rearrange("p t (h d) -> p t h d", h=HG), rows[:, :, :, 0:DH],
                                            rd.unsqueeze(3).broadcast_to([P, CT, HG, DH]),
                                            ALU.mult).then_inc(a.sm_free, 1)

            dve.sem_inc(a.ot_turned, 2)
            for n, item in enumerate(a.before):
                side(0, n, n % 2, item)

            def body(it, last):
                for g in range(G):
                    for s in range(ns):
                        for n, slot, item in a.side(it, last, g, s):
                            side(it, n, slot, item)

            ns = a.ns
            batches(dve, body)

        def attention_pool(pool, a, extra):
            def values(b, g):
                nc.gpsimd.tensor_copy(VR[:, g, :, :].unsqueeze(1),
                                      V[:, bass.ds(b, 1), :, g * HG * VW:(g + 1) * HG * VW]).then_inc(a.values, 1)

            for g in range(G):
                values(0, g)
            extra(pool)
            with pool.Fori(0, B - 1) as it:
                for g in range(G):
                    wait_apart(pool, a.pv_done, it * (G * a.ns) + ((g + 1) * a.ns + 1))
                    values(it + 1, g)

        def attention_sp(sp, a):
            def load(b, g):
                heads = slice(g * HG, (g + 1) * HG)
                for i in range(SPLIT):
                    for j in range(SPLIT):
                        r = (SPLIT * i + j) * DH
                        sp.dma_start(QA[r:r + DH, g, :, :].rearrange("d h t -> d (h t)"),
                                     qs[a.layer][bass.ds(b, 1), i, :, heads, :].rearrange("a d h t -> (a d) (h t)"))\
                            .then_inc(a.loaded[g], 16)
                    r = SPLIT * i * DH
                    sp.dma_start(KA[r:r + SPLIT * DH, g, :, :].rearrange("d h t -> d (h t)"),
                                 ks[a.layer][bass.ds(b, 1), :, :, heads, :].rearrange("a s d h t -> (a s d) (h t)"))\
                        .then_inc(a.loaded[g], 16)

            def maxima(g, n):
                sp.wait_ge(a.sm_free, n + 1)
                for i in range(SPLIT):
                    sp.dma_start(QA[R_MAX + i:R_MAX + i + 1, g, :, :].rearrange("a h (q t) -> a (h q) t", t=P),
                                 MT[i * HG * KT:(i + 1) * HG * KT, g, :]).then_inc(a.maxed[g], 16)

            for g in range(G):
                load(0, g)
            maxima(0, len(a.pieces))

            def body(it, last):
                for g in range(G):
                    for s in range(a.ns):
                        for n, _, item in a.side(it, last, g, s):
                            if item[0] == "rows":
                                maxima(item[1] % G, n)
                    if not last:
                        sp.wait_ge(a.exp_done, it * (2 * G * a.ns) + 2 * (g + 1) * a.ns)
                        load(it + 1, g)

            batches(sp, body)

        def butterflies(pool):
            done = [0]

            def settle():
                pool.wait_ge(bfly, done[0])

            def op(dst, a, b, f):
                nc.gpsimd.tensor_tensor(dst, a, b, f).then_inc(bfly, 1)
                done[0] += 1

            def stage(stage, tensors, w, crossed):
                s = 2 ** stage
                wv = w.rearrange("p (n s k) -> p n s k", s=s, k=4)
                for src, dst, rows in tensors:
                    v = src.rearrange("p (n k s) -> p n k s", k=2, s=s)
                    o = dst.rearrange("p (n k s) -> p n k s", k=2, s=s)
                    t = [TMP[0:rows, i, :].rearrange("p (n s) -> p n s", s=s) for i in range(4)]
                    for i, (k, l) in enumerate(((0, 0), (1, 1), (2, 0), (3, 1))):
                        if crossed:
                            k = {0: 0, 1: 2, 2: 1, 3: 3}[k]
                        op(t[i], wv[0:rows, :, :, k], v[0:rows, :, l, :], ALU.mult)
                    settle()
                    op(o[0:rows, :, 0, :], t[0], t[1], ALU.add)
                    op(o[0:rows, :, 1, :], t[2], t[3], ALU.add)
                    settle()

            n = 0
            for i in range(STAGES):
                pool.wait_ge(bfly_in[n % 2], 16 * (n // 2 + 1))
                last = i == STAGES - 1
                stage(i, [(YW[:, i % 2, :], WUP[:, :] if last else YW[:, (i + 1) % 2, :], P),
                          (YB[:, i % 2, :], BEFF[:, :] if last else YB[:, (i + 1) % 2, :], 1)],
                      WST[:, n % 2, :], False)
                pool.sem_inc(folded, 1)
                n += 1
            for i in range(STAGES):
                pool.wait_ge(bfly_in[n % 2], 16 * (n // 2 + 1))
                last = i == STAGES - 1
                stage(STAGES - 1 - i, [(YC[:, i % 2, :], WDNT[:, :] if last else YC[:, (i + 1) % 2, :], P)],
                      WST[:, n % 2, :], True)
                pool.sem_inc(folded, 1)
                n += 1

        def butterfly_loads(act):
            act.dma_start(YW[:, 0, :], w_exp).then_inc(consts_in, 16)
            act.dma_start(YB[0:1, 0, :], b_exp).then_inc(consts_in, 16)
            act.dma_start(YC[:, 0, :], w_con_t).then_inc(consts_in, 16)
            for n in range(2 * STAGES):
                if n >= 2:
                    act.wait_ge(folded, n - 1)
                src = up_w[n:n + 1, :] if n < STAGES else down_w[2 * STAGES - 1 - n:2 * STAGES - n, :]
                act.dma_start(WST[:, n % 2, :], src.broadcast_to([P, 4 * HID // 2])).then_inc(bfly_in[n % 2], 16)

        @block.sync
        def _(sp):
            for b in range(B):
                sp.dma_start(X[:, b * KT:(b + 1) * KT, :], x[b, :, :].rearrange("(t p) d -> p t d", p=P))\
                    .then_inc(x_in, 16)
            sp.dma_start(ID[:, :], ident).then_inc(x_in, 16)
            sp.dma_start(WQKV[:, :, :], wqkv).then_inc(x_in, 16)
            sp.dma_start(BQK[:, :], bqk).then_inc(x_in, 16)
            sp.dma_start(BV[:, :], bv.broadcast_to([P, D])).then_inc(x_in, 16)
            chunks_sp(sp, CA)
            end_phase(sp, 1)
            for g in range(G):
                for h in range(HG):
                    sp.dma_start(KA[R_SPLIT:R_ALL, g, h, :], alibi_k).then_inc(setup, 16)
                sp.dma_start(QA[R_SPLIT:R_MAX, g, :, :], alibi_q[0, :, g * HG:(g + 1) * HG, :]).then_inc(setup, 16)
            for dst, src in ((DIST[:, :, :], dist), (MASK[:, :, :], mask), (IDB[:, :], identb),
                             (DOWN, down_t), (UP[:, :, :], up), (SIGN[:, :], sign.broadcast_to([P, DH])),
                             (COS[:, :], cos), (SIN[:, :], sin), (WOUT[:, 0, :], wout_a), (WOUT[:, 1, :], wout_b),
                             (BOUT[:, :], bout.broadcast_to([P, D])), (UPB[:, :], up_bias),
                             (FB[:, 0, :], b_con.broadcast_to([P, D])), (FB[:, 1, :], down_bias.broadcast_to([P, D]))):
                sp.dma_start(dst, src).then_inc(setup, 16)
            sp.wait_ge(setup, 16 * (G * (HG + 1) + 14))
            end_phase(sp, 2)
            end_phase(sp, 3)
            attention_sp(sp, AA)
            end_phase(sp, 4)
            for g in range(G):
                sp.dma_start(QA[R_SPLIT:R_MAX, g, :, :], alibi_q[1, :, g * HG:(g + 1) * HG, :]).then_inc(setup, 16)
            sp.wait_ge(setup, 16 * (G * (HG + 2) + 14))
            end_phase(sp, 5)
            chunks_sp(sp, CB)
            end_phase(sp, 6)
            attention_sp(sp, AB)
            end_phase(sp, 7)
            chunks_sp(sp, CC)

        @block.gpsimd
        def _(pool):
            nc.gpsimd.memset(HALF[:, :], -0.5).then_inc(fold, 1)
            nc.gpsimd.memset(V[:, :, :, :].rearrange("p b k (h w) -> p (b k h) w", w=VW)[:, :, DH:VW], 1.0)
            nc.gpsimd.memset(MX[:, :, :, :], -3.0e38)
            nc.gpsimd.memset(BD[:, :, :, :], 0.0).then_inc(fold, 1)
            pool.wait_ge(fold, 2)
            chunks_pool(pool, CA)
            end_phase(pool, 1)
            end_phase(pool, 2)
            end_phase(pool, 3)

            def extra(pool):
                nc.gpsimd.tensor_tensor(FB[:, 0, :], FB[:, 0, :], FB[:, 1, :], ALU.add)
                pool.wait_ge(consts_in, 48)
                butterflies(pool)

            attention_pool(pool, AA, extra)
            end_phase(pool, 4)
            nc.gpsimd.memset(MX[:, :, :, :], -3.0e38)
            end_phase(pool, 5)
            chunks_pool(pool, CB)
            end_phase(pool, 6)
            attention_pool(pool, AB, lambda pool: None)
            end_phase(pool, 7)
            chunks_pool(pool, CC)

        @block.scalar
        def _(act):
            chunks_act(act, CA)
            end_phase(act, 1)
            end_phase(act, 2)
            act.wait_ge(folded_pe, 1)
            nc.scalar.copy(WB[:, 0:4, :], PS[:, 0, :].rearrange("p (k d) -> p k d", k=4))
            nc.scalar.copy(WB[:, 4, :], PS[:, 1, 0:P])
            end_phase(act, 3)
            butterfly_loads(act)
            attention_act(act, AA)
            end_phase(act, 4)
            act.wait_ge(folded_pe, 2)
            nc.scalar.copy(WDN[:, :, :], PS[:, 0, :].rearrange("p (n d) -> p n d", n=HC))
            end_phase(act, 5)
            chunks_act(act, CB)
            end_phase(act, 6)
            attention_act(act, AB)
            end_phase(act, 7)
            chunks_act(act, CC)


        @block.vector
        def _(dve):
            dve.wait_ge(x_in, 16 * X_LOADS)
            chunks_dve(dve, CA)
            end_phase(dve, 1)
            end_phase(dve, 2)
            dve.wait_ge(fold, 2)
            for kind in (1, 3):
                s = nc.vector.tensor_tensor(UP[:, kind, :], UP[:, kind, :], SIGN[:, :], ALU.mult)
            s.then_inc(fold, 1)
            dve.wait_ge(fold, 3)
            for half in range(2):
                rows = slice(half * LAT, (half + 1) * LAT)
                s = nc.vector.tensor_copy(BD[rows, :, half, :], UP[rows, :, :])
            s.then_inc(fold, 1)
            end_phase(dve, 3)
            attention_dve(dve, AA)
            end_phase(dve, 4)
            dve.wait_ge(folded_pe, 2)
            nc.vector.tensor_tensor(BUP[:, :], PS[:, 1, 0:HC], UPB[:, :], ALU.add)
            end_phase(dve, 5)
            chunks_dve(dve, CB)
            end_phase(dve, 6)
            attention_dve(dve, AB)
            end_phase(dve, 7)
            chunks_dve(dve, CC)

        @block.tensor
        def _(pe):
            pe.wait_ge(x_in, 16 * X_LOADS)
            chunks_pe(pe, CA)
            end_phase(pe, 1)
            end_phase(pe, 2)
            pe.wait_ge(fold, 4)
            for kind in range(5):
                for j in range(D // (2 * DH)):
                    to = PS[:, kind // 4, (kind % 4) * P:(kind % 4 + 1) * P]
                    to = to.rearrange("p (d h) -> p h d", h=H) if kind < 4 else to.rearrange("p (h d) -> p h d", h=H)
                    mm = pe.matmul(to[:, 2 * j:2 * j + 2, :],
                                   DOWN[:, (0, 0, 1, 1, 2)[kind], j, :],
                                   BD[:, kind, :, :], start=True, stop=True)
            mm.then_inc(folded_pe, 1)
            end_phase(pe, 3)
            attention_pe(pe, AA)
            end_phase(pe, 4)
            for n in range(HC):
                pe.transpose(PS[:, 0, n * P:(n + 1) * P], WDNT[:, n * P:(n + 1) * P], ID[:, :])
            for n in range(HC):
                mm = pe.matmul(PS[:, 1, n:n + 1], BEFF[0:1, n * P:(n + 1) * P], ID[0:1, 0:1], start=True, stop=True)
            mm.then_inc(folded_pe, 1)
            end_phase(pe, 5)
            chunks_pe(pe, CB)
            end_phase(pe, 6)
            attention_pe(pe, AB)
            end_phase(pe, 7)
            chunks_pe(pe, CC)


def _alibi():
    i = np.arange(T)
    blk, low = i // P, i % P
    slope = 0.5 ** np.arange(H)
    c = np.arange(KT)[:, None]
    far = -np.abs(blk[None] - c) * P
    near = -np.sign(blk[None] - c) * low[None]
    hot = (blk[None] == c).astype(float)
    q = np.stack([far, near, hot]).reshape(R_BIAS, 1, T) * slope[None, :, None]
    q = np.stack([q, 0 * q])
    k = np.concatenate([hot, hot, np.sign(c - blk[None]) * low[None], np.ones((SPLIT, T))])
    j = np.arange(P)
    dist = -np.abs(j[:, None] - j[None])[:, None, :] * slope[None, :, None]
    late = (j[:, None] > j[None]) * -BIG
    mask = np.stack([late, late.T], 1)
    return q, k, dist, mask


def _rope():
    dim = DH // 2
    inv = (np.float32(1.0) / np.float32(10000.0) ** (np.arange(0, dim, 2, dtype=np.float32) / np.float32(dim)))
    freqs = np.arange(T, dtype=np.float32)[:, None] * inv.astype(np.float32)[None, :]
    emb = np.concatenate([freqs, freqs], -1).T
    cos = np.ones((DH, T), np.float32)
    sin = np.zeros((DH, T), np.float32)
    cos[DH // 2:] = np.cos(emb)
    sin[DH // 2:] = np.sin(emb)
    return np.repeat(cos, H, 0), np.repeat(sin, H, 0)


def kernel(**inputs):
    import numpy as np
    import ml_dtypes
    import concourse.bacc as bacc
    from concourse.bass_utils import run_bass_kernel_spmd

    a = {k.removeprefix("L0_"): np.asarray(v) for k, v in inputs.items()}
    bf = ml_dtypes.bfloat16
    q_bias, k_bias, dist, mask = _alibi()
    cos, sin = _rope()
    w, wb = a["attn_a_qkv_w"].reshape(H, 3, DH, D), a["attn_a_qkv_b"].reshape(H, 3, DH)
    qkv = np.stack([w[:, 0].transpose(2, 1, 0).reshape(D, D), w[:, 1].transpose(2, 1, 0).reshape(D, D),
                    w[:, 2].transpose(2, 0, 1).reshape(D, D)], 1)
    qkv_b = np.stack([wb[:, 0].T.reshape(D), wb[:, 1].T.reshape(D), wb[:, 2].reshape(D)])

    def down(name):
        return a[name].T.reshape(D // (2 * DH), P, D).transpose(1, 0, 2)

    def up(c, e):
        return np.concatenate([a[c], a[e]], 1)

    swap = [1, 0, 3, 2]
    q_up, k_up = up("attn_b_Wq_up_c", "attn_b_Wq_up_e"), up("attn_b_Wk_up_c", "attn_b_Wk_up_e")

    def swapped(u):
        return np.concatenate([u[:, :4], u[:, 4:][:, swap]], 1)

    ups = np.stack([q_up, swapped(q_up), k_up, swapped(k_up), a["attn_b_Wv_up"]], 1)
    arrays = {
        "x": a["attn_a_x"], "wqkv": qkv, "bqk": qkv_b[:2].T, "bv": qkv_b[2:3],
        "wout_a": a["attn_a_out_w"].T, "bout": a["attn_a_out_b"][None],
        "ident": np.eye(P, dtype=np.float32), "identb": np.eye(P).astype(bf),
        "alibi_q": q_bias.astype(bf), "alibi_k": k_bias.astype(bf), "dist": dist.astype(bf), "mask": mask.astype(bf),
        "down_t": np.stack([down("attn_b_Wq_down"), down("attn_b_Wk_down"), down("attn_b_Wv_down")], 1),
        "up": np.concatenate([ups, ups]), "sign": np.array([[0, 0, 0, 0, -1, 1, -1, 1]], np.float32),
        "cos": cos, "sin": sin, "wout_b": a["attn_b_Wc"],
        "w_exp": a["ffn_W_exp"], "b_exp": a["ffn_b_exp"][None],
        "up_w": a["ffn_up_weights"].reshape(STAGES, -1), "up_bias": a["ffn_up_bias"].reshape(HC, P).T,
        "down_w": a["ffn_down_weights"].reshape(STAGES, -1), "w_con_t": a["ffn_W_con"].T,
        "b_con": a["ffn_b_con"][None], "down_bias": a["ffn_down_bias"][None],
    }
    arrays = {f"in_{k}": np.ascontiguousarray(v) for k, v in arrays.items()}
    nc = bacc.Bacc("TRN2", target_bir_lowering=False, num_devices=1)
    args = {k[3:]: nc.dram_tensor(k, v.shape, mybir.dt.from_np(v.dtype), kind="ExternalInput").ap()
            for k, v in arrays.items()}
    out = nc.dram_tensor("out", (B, T, D), F32, kind="ExternalOutput").ap()
    build(nc, out=out, **args)
    result = run_bass_kernel_spmd(nc, [arrays], core_ids=[0])
    return result.results[0]["out"]
```

```python
from contextlib import ExitStack

import numpy as np

import concourse.bass as bass
from concourse import mybir

P = 128
B = 4
T = 1024
D = 128
H = 16
DH = D // H
HG = 4
G = H // HG
KT = T // P
CH = 512
CT = CH // P
NC = T // CH
HID = 512
HC = HID // P
STAGES = 9
LAT = 64
VW = DH + 1
SPLIT = 3
R_SPLIT = SPLIT * SPLIT * DH
R_BIAS = 3 * KT
R_MAX = R_SPLIT + R_BIAS
R_ALL = R_MAX + SPLIT
LEAD = 16
ROWS_LAG = 6
SIDES = 3
EPS = 1e-5
SCALE = float(np.float32(1.0) / np.sqrt(np.float32(DH)))
BIG = 1e30

F32 = mybir.dt.float32
BF16 = mybir.dt.bfloat16
ALU = mybir.AluOpType
ACT = mybir.ActivationFunctionType
AX_X = mybir.AxisListType.X


def attention_plan(causal):
    steps, pieces = [], []
    for qc in range(NC):
        for kb in range(KT):
            lo = max(0, kb * P - qc * CH) if causal else 0
            if lo < CH:
                steps.append((qc, kb, lo))
    for h in range(HG):
        for qt in range(KT):
            for half in range(NC):
                width = min(CH, (qt + 1) * P - half * CH) if causal else CH
                if width > 0:
                    at = qt * P - half * CH
                    pieces.append((h, qt, half, width, at if 0 <= at < width else None))
    return steps, pieces


def build(nc, x, out, wqkv, bqk, bv, wout_a, bout, ident, identb, alibi_q, alibi_k, dist, mask,
          down_t, up, sign, cos, sin, wout_b, w_exp, b_exp, up_w, up_bias, down_w, w_con_t, b_con,
          down_bias):
    ctx = ExitStack()
    with ctx:
        def sb(name, shape, dt=F32):
            return ctx.enter_context(nc.sbuf_tensor(name, shape, dt))

        def sem(name):
            return ctx.enter_context(nc.semaphore(name))

        def sems(name, n):
            return [sem(f"{name}{i}") for i in range(n)]

        def dram(name, shape, dt):
            return nc.dram_tensor(name, shape, dt, kind="Internal").ap()

        X = sb("X", [P, B * KT, D])
        O = sb("O", [P, B * KT, D])
        V = sb("V", [P, B, KT, H * VW])
        QA = sb("QA", [R_ALL, G, HG, T], BF16)
        KA = sb("KA", [R_ALL, G, HG, T], BF16)
        VR = sb("VR", [P, G, KT, HG * VW])
        DIST = sb("DIST", [P, H, P], BF16)
        MASK = sb("MASK", [P, 2, P], BF16)
        IDB = sb("IDB", [P, P], BF16)
        ID = sb("ID", [P, P])
        MX = sb("MX", [P, 2, HG * KT, NC])
        NM = sb("NM", [P, 3, HG * KT])
        MP = sb("MP", [P, 2, SPLIT, HG * KT], BF16)
        MT = sb("MT", [SPLIT * HG * KT, G, P], BF16)
        OT = sb("OT", [P, NC, CH])
        RD = sb("RD", [P, 2, CT * HG])
        WQKV = sb("WQKV", [P, 3, D])
        BQK = sb("BQK", [P, 2])
        BV = sb("BV", [P, D])
        WOUT = sb("WOUT", [P, 2, D])
        BOUT = sb("BOUT", [P, D])
        WB = sb("WB", [P, 5, D])
        UP = sb("UP", [P, 5, DH])
        SIGN = sb("SIGN", [P, DH])
        BD = sb("BD", [P, 5, 2, DH])
        COS = sb("COS", [P, T])
        SIN = sb("SIN", [P, T])
        WUP = sb("WUP", [P, HID])
        BUP = sb("BUP", [P, HC])
        UPB = sb("UPB", [P, HC])
        WDNT = sb("WDNT", [P, HID])
        WDN = sb("WDN", [P, HC, D])
        BEFF = sb("BEFF", [1, HID])
        FB = sb("FB", [P, 2, D])
        HALF = sb("HALF", [P, CT])
        CHAIN = 10 * CH
        WORK = sb("WORK", [P, 2 * CHAIN])
        ROT = WDNT
        SPL = sb("SPL", [P, 2, 2, SPLIT, CH], BF16)
        STATS = sb("STATS", [P, 2, CT, 6])
        MV = sb("MV", [P, 2, CT, 2])
        VE = sb("VE", [P, 2, CT])
        RS = sb("RS", [P, 2, CT])

        def work(j, at, n=1):
            return WORK[:, j * CHAIN + at * CH:j * CHAIN + (at + n) * CH]

        xn = [work(j, 0) for j in range(2)]
        xt = [work(j, 1) for j in range(2)]
        os_ = [work(j, 2) for j in range(2)]
        ott = [work(j, 3) for j in range(2)]
        gel = [work(j, 4, HC) for j in range(2)]
        q32 = [work(j, 8) for j in range(2)]
        rest = [work(j, 9) for j in range(2)]
        PR = WORK[:, 0:4 * 2 * CH].rearrange("p (s h q) -> p s h q", s=4, h=2)
        DOWN = O[:, 0:3 * 8, :].rearrange("p (k j) c -> p k j c", k=3)
        at = 8 * CH
        WST = WORK[:, at:at + 4 * CH].rearrange("p (b w) -> p b w", b=2)
        TMP = WORK[:, at + 4 * CH:at + 6 * CH].rearrange("p (b w) -> p b w", b=4)
        YW = WORK[:, at + 6 * CH:at + 8 * CH].rearrange("p (b w) -> p b w", b=2)
        YB = WORK[:, at + 8 * CH:at + 10 * CH].rearrange("p (b w) -> p b w", b=2)
        YC = WORK[:, at + 10 * CH:at + 12 * CH].rearrange("p (b w) -> p b w", b=2)

        PS = ctx.enter_context(nc.psum_tensor("PS", [P, 8, CH], F32))
        SM_BANK, OT_BANK = 4, 7

        qs = [dram(f"qs{i}", [B, SPLIT, DH, H, T], BF16) for i in range(2)]
        ks = [dram(f"ks{i}", [B, SPLIT, DH, H, T], BF16) for i in range(2)]

        x_in = sem("x_in")
        consts_in = sem("consts_in")
        bias_rows_in = sem("bias_rows_in")
        phase = sem("phase")
        setup = sem("setup")
        apart = sem("apart")
        fold = sem("fold")
        folded_pe = sem("folded_pe")
        bfly_in = sems("bfly_in", 2)
        bfly = sem("bfly")
        out_sem = sem("out_sem")

        block = ctx.enter_context(nc.Block())
        ENGINES = 5
        X_LOADS = B + 4

        def wait_apart(e, s, value):
            e.wait_ge(s, value)
            e.sem_inc(apart, 1)

        def end_phase(e, n):
            e.drain().then_inc(phase, 1)
            e.wait_ge(phase, ENGINES * n)

        class Chunks:

            def __init__(self, name, layer, attended, ffn, project):
                self.layer, self.attended, self.ffn, self.project = layer, attended, ffn, project
                self.norms = 2 if ffn and project is not None else 1
                self.turns = self.norms + attended
                self.first_wide = HC if ffn else 0
                self.projections = (0 if project is None else (2 if project == 0 else 4))
                self.wides = self.first_wide + self.projections
                self.split = 4 if project == 0 else 5
                self.lag = 2 if ffn else 1

                def two(signal, used=True):
                    return sems(f"{name}_{signal}", 2) if used else None

                self.o_copied = two("o_copied", attended)
                self.x_biased = two("x_biased", attended and layer == 0)
                self.ffn_biased = two("ffn_biased", ffn)
                self.x_added = two("x_added", attended)
                self.stats_done = two("stats_done")
                self.mv_done = two("mv_done")
                self.var_ready = two("var_ready")
                self.rstd_ready = two("rstd_ready")
                self.xn_ready = two("xn_ready")
                self.turn_full = two("turn_full")
                self.turn_free = two("turn_free")
                self.y_full = two("y_full", attended)
                self.y_used = two("y_used", attended)
                self.d_full = two("d_full", ffn)
                self.d_used = two("d_used", ffn)
                self.v_full = two("v_full", project is not None)
                self.v_used = two("v_used", project is not None)
                self.wide_full = two("wide_full")
                self.gelu_done = two("gelu_done", ffn)
                self.proj_used = two("proj_used", project is not None)
                self.split_step = two("split_step", project is not None)
                self.stored = two("stored", project is not None)

        CA = Chunks("pa", 0, 0, 0, 0)
        CB = Chunks("pb", 0, 1, 1, 1)
        CC = Chunks("pc", 1, 1, 1, None)

        def slots(e, c, slot):
            def at(it, k, lag):
                if isinstance(it, int):
                    n = NC * it + k - lag
                    return divmod(n, NC) if 0 <= n < NC * B else None
                back, j = divmod(k - lag, NC)
                return (it + back if back else it), j

            def batch(it):
                for k in range(NC):
                    where = (at(it, k, 0), at(it, k, 1) if c.ffn else None,
                             at(it, k, c.lag) if c.project is not None else None)
                    if any(w is not None for w in where):
                        slot(*where)

            batch(0)
            with e.Fori(1, B) as it:
                batch(it)
            batch(B)

        def bank(j, i):
            return PS[:, 4 * j + i, :]

        def tile0(it, j):
            return it * KT + j * CT

        def blocks(it, j, n=CT, first=0):
            at = tile0(it, j) + first
            return slice(at, at + n) if isinstance(it, int) else bass.ds(at, n)

        def block_of(it):
            return slice(it, it + 1) if isinstance(it, int) else bass.ds(it, 1)

        def chunks_pe(pe, c):
            def turn(it, j, i, src):
                pe.wait_ge(c.turn_free[j], it * c.turns + (i + 1))
                for t in range(CT):
                    mm = pe.transpose(bank(j, 0)[:, t * P:(t + 1) * P], src[:, t * P:(t + 1) * P], ID[:, :])
                mm.then_inc(c.turn_full[j], 1)

            def normed(it, j, k):
                pe.wait_ge(c.xn_ready[j], it * c.norms + (k + 1))
                turn(it, j, c.attended + k, xn[j])

            def wide(it, j, n, lhs):
                m, own = (n - 2, 1) if n >= 2 else (n - 2 + c.wides, 0)
                if m < c.first_wide:
                    pe.wait_ge(c.gelu_done[j], it * HC + (own * HC + m + 1))
                else:
                    pe.wait_ge(c.proj_used[j], it * c.projections
                               + (own * c.projections + m - c.first_wide + 1))
                pe.matmul(bank(j, 2 + n % 2), lhs, xt[j], start=True, stop=True).then_inc(c.wide_full[j], 1)

            def rows(it, j, src, weights, full):
                for t in range(CT):
                    mm = pe.matmul(bank(j, 1)[:, t * P:(t + 1) * P], src[j][:, t * P:(t + 1) * P], weights,
                                   start=True, stop=True)
                mm.then_inc(full[j], 1)

            def slot(first, second, third):
                if first and c.attended:
                    it, j = first
                    pe.wait_ge(c.o_copied[j], it + 1)
                    turn(it, j, 0, os_[j])
                if second:
                    it, j = second
                    pe.wait_ge(c.turn_free[j], it * c.turns + (c.attended + 2))
                    for n in range(HC):
                        wide(it, j, n, WUP[:, n * P:(n + 1) * P])
                if first and c.attended:
                    it, j = first
                    pe.wait_ge(c.turn_free[j], it * c.turns + 2)
                    pe.wait_ge(c.d_used[j], it + 1)
                    rows(it, j, ott, WOUT[:, c.layer, :], c.y_full)
                if second:
                    it, j = second
                    if c.v_used is not None:
                        pe.wait_ge(c.v_used[j], it + 1)
                    pe.wait_ge(c.y_used[j], it + 2)
                    pe.wait_ge(c.gelu_done[j], it * HC + 2 * HC)
                    for t in range(CT):
                        for n in range(HC):
                            mm = pe.matmul(bank(j, 1)[:, t * P:(t + 1) * P],
                                           gel[j][:, n * CH + t * P:n * CH + (t + 1) * P],
                                           WDN[:, n, :], start=(n == 0), stop=(n == HC - 1))
                    mm.then_inc(c.d_full[j], 1)
                if third:
                    it, j = third
                    pe.wait_ge(c.turn_free[j], it * c.turns + (c.turns + 1))
                    for k in range(c.wides - c.first_wide):
                        wide(it, j, c.first_wide + k, WQKV[:, k, :] if c.project == 0 else WB[:, k, :])
                    pe.wait_ge(c.v_used[j], it + 1)
                    if c.ffn:
                        pe.wait_ge(c.d_used[j], it + 2)
                        if isinstance(it, int) and it == B - 1:
                            pe.wait_ge(c.y_used[j], it + 2)
                        else:
                            pe.wait_ge(c.y_used[j], it + 3)
                    rows(it, j, xt, WQKV[:, 2, :] if c.project == 0 else WB[:, 4, :], c.v_full)
                if first:
                    normed(*first, 0)
                if second and c.norms == 2:
                    normed(*second, 1)

            for j in range(2):
                for s in (c.y_full, c.d_full, c.v_full):
                    if s is not None:
                        pe.sem_inc(s[j], 1)
            slots(pe, c, slot)

        def chunks_act(act, c):
            def turn(it, j, i, dst, readers):
                act.wait_ge(c.turn_full[j], it * c.turns + (i + 1))
                if readers is not None:
                    act.wait_ge(readers[j], it + 1)
                nc.scalar.copy(dst, bank(j, 0)).then_inc(c.turn_free[j], 1)

            def slot(first, second, third):
                if first and c.attended:
                    turn(*first, 0, ott[first[1]], c.y_full)
                if second:
                    it, j = second
                    for n in range(HC):
                        act.wait_ge(c.wide_full[j], it * c.wides + (n + 1))
                        if n == 0:
                            act.wait_ge(c.d_full[j], it + 1)
                        nc.scalar.activation(gel[j][:, n * CH:(n + 1) * CH], bank(j, 2 + n % 2), ACT.Gelu,
                                             bias=BUP[:, n:n + 1]).then_inc(c.gelu_done[j], 1)
                if third and c.project == 1:
                    it, j = third
                    act.wait_ge(c.v_full[j], it + 2)
                    nc.scalar.copy(values_of(it, j), bank(j, 1).rearrange("p (t h d) -> p t h d", t=CT, h=H))\
                        .then_inc(c.v_used[j], 1)
                if first:
                    turn(*first, c.attended, xt[first[1]], None if c.project is None else c.v_full)
                if second and c.norms == 2:
                    turn(*second, c.attended + 1, xt[second[1]], None)

            for j in range(2):
                act.sem_inc(c.turn_free[j], 1)
                if c.ffn:
                    act.sem_inc(c.gelu_done[j], HC)
            slots(act, c, slot)

        def values_of(it, j):
            return V[:, block_of(it), j * CT:(j + 1) * CT, :]\
                .rearrange("p a t (h w) -> p (a t) h w", h=H)[:, :, :, 0:DH]

        def chunks_pool(pool, c):
            def power(it, j, k):
                pool.wait_ge(c.var_ready[j], it * c.norms + (k + 1))
                nc.gpsimd.tensor_tensor(RS[:, j, :], VE[:, j, :], HALF[:, :], ALU.pow).then_inc(c.rstd_ready[j], 1)

            def bias(it, j, row, sem_):
                xs = X[:, blocks(it, j), :]
                nc.gpsimd.tensor_tensor(xs, xs, row.unsqueeze(1).broadcast_to([P, CT, D]),
                                        ALU.add).then_inc(sem_[j], 1)

            def slot(first, second, third):
                if first and c.attended:
                    it, j = first
                    wait_apart(pool, c.turn_free[j], it * c.turns + 1)
                    nc.gpsimd.tensor_copy(os_[j].rearrange("p (t d) -> p t d", t=CT),
                                          O[:, blocks(it, j), :]).then_inc(c.o_copied[j], 1)
                    if c.layer == 0:
                        bias(it, j, BOUT[:, :], c.x_biased)
                if first:
                    power(*first, 0)
                if first and c.ffn:
                    it, j = first
                    wait_apart(pool, c.xn_ready[j], it * c.norms + 1)
                    bias(it, j, FB[:, 0, :], c.ffn_biased)
                if second and c.norms == 2:
                    power(*second, 1)

            slots(pool, c, slot)

        def chunks_dve(dve, c):
            adds = c.attended + c.ffn

            def add(it, j, k, full, used, biased):
                dve.wait_ge(full[j], it + 2)
                if biased is not None:
                    dve.wait_ge(biased[j], it + 1)
                xs = X[:, blocks(it, j), :]
                nc.vector.tensor_tensor(xs, bank(j, 1).rearrange("p (t d) -> p t d", t=CT), xs,
                                        ALU.add).then_inc(c.x_added[j], 1)
                dve.wait_ge(c.x_added[j], it * adds + (k + 1))
                dve.sem_inc(used[j], 1)

            def row_of(it, j, t):
                return X[:, blocks(it, j, 1, t), :].rearrange("p a d -> p (a d)")

            def stats(it, j, k):
                for t in range(CT):
                    s = nc.vector.bn_stats(STATS[:, j, t, :], row_of(it, j, t))
                s.then_inc(c.stats_done[j], 1)
                wait_apart(dve, c.stats_done[j], it * c.norms + (k + 1))
                for t in range(CT):
                    s = nc.vector.bn_aggr(MV[:, j, t, :], STATS[:, j, t, :])
                s.then_inc(c.mv_done[j], 1)
                dve.wait_ge(c.mv_done[j], it * c.norms + (k + 1))
                nc.vector.tensor_scalar(VE[:, j, :], MV[:, j, :, 1], EPS, None, ALU.add).then_inc(c.var_ready[j], 1)

            def norm(it, j, k):
                dve.wait_ge(c.rstd_ready[j], it * c.norms + (k + 1))
                dve.wait_ge(c.turn_free[j], it * c.turns + (c.attended + k + 1))
                for t in range(CT):
                    s = nc.vector.tensor_scalar(xn[j][:, t * P:(t + 1) * P], row_of(it, j, t),
                                                MV[:, j, t, 0:1], RS[:, j, t:t + 1], ALU.subtract, ALU.mult)
                s.then_inc(c.xn_ready[j], 1)

            def project(it, j, qk):
                if qk == 0:
                    dve.wait_ge(c.stored[j], it * 32 + 1)
                scale = SCALE if qk == 0 else 1.0
                step = it * 2 * c.split
                s0 = qk * c.split
                if c.project == 0:
                    n = c.first_wide + qk
                    dve.wait_ge(c.wide_full[j], it * c.wides + (n + 1))
                    nc.vector.tensor_scalar(q32[j], bank(j, 2 + n % 2), BQK[:, qk:qk + 1], scale,
                                            ALU.add, ALU.mult).then_inc(c.proj_used[j], 1)
                    dve.wait_ge(c.proj_used[j], it * c.projections + (c.projections + qk + 1))
                else:
                    cols = slice(j * CH, (j + 1) * CH)
                    for i, (dst, table) in enumerate(((rest[j], COS), (ROT[:, :], SIN))):
                        n = c.first_wide + 2 * qk + i
                        dve.wait_ge(c.wide_full[j], it * c.wides + (n + 1))
                        nc.vector.scalar_tensor_tensor(out=dst, in0=bank(j, 2 + n % 2), scalar=scale,
                                                       in1=table[:, cols], op0=ALU.mult,
                                                       op1=ALU.mult).then_inc(c.proj_used[j], 1)
                    dve.wait_ge(c.proj_used[j], it * c.projections + (c.projections + 2 * qk + 2))
                    nc.vector.tensor_tensor(q32[j], rest[j], ROT[:, :], ALU.add).then_inc(c.split_step[j], 1)
                    s0 += 1
                    dve.wait_ge(c.split_step[j], step + s0)
                for dst, a, b in ((SPL[:, j, qk, 0, :], q32[j], None),
                                  (rest[j], q32[j], SPL[:, j, qk, 0, :]),
                                  (SPL[:, j, qk, 1, :], rest[j], None),
                                  (SPL[:, j, qk, 2, :], rest[j], SPL[:, j, qk, 1, :])):
                    if b is None:
                        s = nc.vector.tensor_copy(dst, a)
                    else:
                        s = nc.vector.tensor_tensor(dst, a, b, ALU.subtract)
                    s.then_inc(c.split_step[j], 1)
                    s0 += 1
                    dve.wait_ge(c.split_step[j], step + s0)

            def values(it, j):
                dve.wait_ge(c.v_full[j], it + 2)
                nc.vector.tensor_tensor(values_of(it, j), bank(j, 1).rearrange("p (t h d) -> p t h d", t=CT, h=H),
                                        BV[:, :].rearrange("p (h d) -> p h d", h=H).unsqueeze(1)
                                        .broadcast_to([P, CT, H, DH]), ALU.add).then_inc(c.v_used[j], 1)

            def slot(first, second, third):
                if first:
                    if c.attended:
                        add(*first, 0, c.y_full, c.y_used, c.x_biased if c.layer == 0 else None)
                    stats(*first, 0)
                    norm(*first, 0)
                if second:
                    add(*second, 1, c.d_full, c.d_used, c.ffn_biased)
                    if c.norms == 2:
                        stats(*second, 1)
                if third:
                    project(*third, 0)
                if second and c.norms == 2:
                    norm(*second, 1)
                if third:
                    project(*third, 1)
                    if c.project == 0:
                        values(*third)

            for j in range(2):
                for s in (c.y_used, c.d_used, c.v_used):
                    if s is not None:
                        dve.sem_inc(s[j], 1)
                if c.project is not None:
                    dve.sem_inc(c.proj_used[j], c.projections)
            slots(dve, c, slot)

        def chunks_sp(sp, c):
            def slot(first, second, third):
                if c.project is None and second:
                    it, j = second
                    sp.wait_ge(c.x_added[j], it * 2 + 2)
                    sp.dma_start(out[block_of(it), j * CH:(j + 1) * CH, :]
                                 .rearrange("a (t p) d -> p (a t) d", p=P),
                                 X[:, blocks(it, j), :]).then_inc(out_sem, 16)
                if third:
                    it, j = third
                    for qk, scratch in enumerate((qs[c.project], ks[c.project])):
                        sp.wait_ge(c.split_step[j], it * 2 * c.split + (qk + 1) * c.split)
                        sp.dma_start(scratch[block_of(it), :, :, :, j * CH:(j + 1) * CH]
                                     .rearrange("a s d h t -> (d h) (a s) t"),
                                     SPL[:, j, qk, :, :]).then_inc(c.stored[j], 16)

            if c.project is not None:
                for j in range(2):
                    sp.sem_inc(c.stored[j], 1)
            slots(sp, c, slot)
            for j in range(2):
                if c.project is not None:
                    sp.wait_ge(c.stored[j], 32 * B + 1)
            if c.project is None:
                sp.wait_ge(out_sem, 16 * NC * B)

        class Attention:
            def __init__(self, layer):
                self.layer = layer
                self.steps, self.pieces = attention_plan(layer == 1)
                self.ns = len(self.steps)
                self.quota = self.shares()
                n = "ab"[layer]
                self.loaded = sems(f"{n}_loaded", G)
                self.maxed = sems(f"{n}_maxed", G)
                self.values = sem(f"{n}_values")
                self.st_full = sem(f"{n}_st_full")
                self.exp_done = sem(f"{n}_exp_done")
                self.pv_done = sem(f"{n}_pv_done")
                self.ot_free = sem(f"{n}_ot_free")
                self.ot_turned = sem(f"{n}_ot_turned")
                self.sm_full = sem(f"{n}_sm_full")
                self.sm_free = sem(f"{n}_sm_free")
                self.parts = sem(f"{n}_parts")
                self.dchain = sem(f"{n}_dchain")
                self.before = [("piece", 0, i) for i in range(len(self.pieces))] + [("rows", 0)]
                self.before += [("piece", 1, i) for i in range(LEAD)]
                self.base = len(self.before)
                self.steady = [(g, s, x) for g in range(G) for s in range(self.ns) for x in self.items(g, s)]
                self.total = len(self.steady)
                self.final = [y for y in self.steady if y[2][0] == "out" or y[2][1] < G]
                steady = [k % SIDES for k in range(self.total)]
                before = steady[-self.base:]
                self.slots_before = self.distances([], before)
                self.slots_steady = self.distances(steady, steady)
                self.slots_final = self.distances(steady, steady[:len(self.final)])

            def distances(self, history, slots):
                whole = history + slots
                result = []
                for k in range(len(history), len(whole)):
                    d = next((d for d in range(1, k + 1) if whole[k - d] == whole[k]), None)
                    result.append((whole[k], d))
                return result

            def shares(self):
                n = len(self.pieces)
                cost = [self.pieces[(i + LEAD) % n][3] + 64 for i in range(n)]
                weight = [(CH - lo) * 2 + (256 if 0 <= kb * P - qc * CH < CH else 0) + 64
                          for qc, kb, lo in self.steps]
                quota, i, spent, done = [], 0, 0, 0
                for w in weight:
                    done += w
                    first = i
                    while i < n and spent + cost[i] / 2 < sum(cost) * done / sum(weight):
                        spent += cost[i]
                        i += 1
                    quota.append(i - first)
                quota[-1] += n - i
                return quota

            def items(self, g, s):
                n = len(self.pieces)
                first = g * n + sum(self.quota[:s]) + LEAD
                items = []
                for p in range(first, first + self.quota[s]):
                    items.append(("piece", p // n + 1, p % n))
                    if p % n == ROWS_LAG - 1:
                        items.append(("rows", p // n))
                half = next(i for i, (qc, _, _) in enumerate(self.steps) if qc == 1)
                if s == half + 3:
                    items.append(("out", g, 0))
                if g and s == 2:
                    items.append(("out", g - 1, 1))
                if g == G - 1 and s == self.ns - 1:
                    items.append(("out", g, 1))
                return items

            def side(self, it, last, g, s):
                items, slots = (self.final, self.slots_final) if last else (self.steady, self.slots_steady)
                return [(it * self.total + (self.base + k), slots[k][0], slots[k][1], x)
                        for k, (gg, ss, x) in enumerate(items) if (gg, ss) == (g, s)]

        AA, AB = Attention(0), Attention(1)

        def batches(e, body):
            with e.Fori(0, B - 1) as it:
                body(it, False)
            body(B - 1, True)

        def unit_of(it, g):
            return (it, g) if g < G else (it + 1, g - G)

        def attention_pe(pe, a):
            ns = a.ns

            def scores(it, g, s, pair, m):
                b, g = unit_of(it, g)
                qc, kb, lo = a.steps[s]
                if s == 0 and pair == 0:
                    pe.wait_ge(a.maxed[g], (b + 1) * 48)
                if m is not None:
                    pe.wait_ge(a.exp_done, m)
                for hh in range(2):
                    h = 2 * pair + hh
                    diagonal = kb * P - qc * CH
                    has = 0 <= diagonal < CH
                    mm = pe.matmul(PS[:, 2 * pair + hh, lo:CH], KA[:, g, h, kb * P:(kb + 1) * P],
                                   QA[:, g, h, qc * CH + lo:(qc + 1) * CH], start=True, stop=not has)
                    if has:
                        block = DIST[:, g * HG + h, :] if a.layer == 0 else MASK[:, 0, :]
                        mm = pe.matmul(PS[:, 2 * pair + hh, diagonal:diagonal + P], IDB[:, :], block,
                                       start=False, stop=True)
                mm.then_inc(a.st_full, 1)

            def weighted(it, g, s):
                qc, kb, lo = a.steps[s]
                t = it * (G * ns) + (g * ns + s)
                if s == 0:
                    pe.wait_ge(a.values, it * G + (g + 1))
                if kb == 0:
                    pe.wait_ge(a.ot_free, it * (G * NC) + (NC * g + qc + 1))
                pe.wait_ge(a.exp_done, t * 2 + 2)
                last = s + 1 == ns or a.steps[s + 1][0] != qc
                for h in range(HG):
                    mm = pe.matmul(PS[32 * h:32 * h + VW, OT_BANK, lo:CH],
                                   VR[:, g, kb, h * VW:(h + 1) * VW],
                                   PR[:, 2 * ((g * ns + s) % 2) + h // 2, h % 2, lo:CH],
                                   start=(kb == 0), stop=last)
                mm.then_inc(a.pv_done, 1)

            def side(n, slot, back, item, it=0):
                kind = item[0]
                if back is not None:
                    pe.wait_ge(a.sm_free, n - (back - 1))
                bank_ = PS[:, SM_BANK + slot, :]
                if kind == "piece":
                    b, g = unit_of(it, item[1])
                    h, qt, half, width, diagonal = a.pieces[item[2]]
                    if item[2] == 0:
                        pe.wait_ge(a.loaded[g], (b + 1) * 16 * SPLIT * (SPLIT + 1))
                    mm = pe.matmul(bank_[:, 0:width], QA[0:R_MAX, g, h, qt * P:(qt + 1) * P],
                                   KA[0:R_MAX, g, h, half * CH:half * CH + width],
                                   start=True, stop=diagonal is None)
                    if diagonal is not None:
                        block = DIST[:, g * HG + h, :] if a.layer == 0 else MASK[:, 1, :]
                        mm = pe.matmul(bank_[:, diagonal:diagonal + P], IDB[:, :], block, start=False, stop=True)
                elif kind == "rows":
                    pe.wait_ge(a.parts, it * G + (item[1] + 1))
                    mm = pe.transpose(bank_.bitcast(BF16)[0:SPLIT * HG * KT, 0:P],
                                      MP[:, item[1] % 2, :, :].rearrange("p s r -> p (s r)"), IDB[:, :])
                else:
                    o = NC * item[1] + item[2]
                    pe.wait_ge(a.ot_free, it * (G * NC) + (o + 2))
                    for t in range(CT):
                        mm = pe.transpose(bank_[:, t * P:(t + 1) * P], OT[:, item[2], t * P:(t + 1) * P], ID[:, :])
                mm.then_inc(a.sm_full, 1)

            pe.sem_inc(a.pv_done, 1)
            for n, item in enumerate(a.before):
                side(n, *a.slots_before[n], item)
            for pair in range(2):
                scores(0, 0, 0, pair, None)

            def body(it, last):
                for g in range(G):
                    for s in range(ns):
                        todo = a.side(it, last, g, s)
                        following = (g, s + 1) if s + 1 < ns else (g + 1, 0)
                        t = it * (G * ns) + (g * ns + s)
                        cuts = [len(todo) * i // 4 for i in range(4)]
                        for pair in range(2):
                            if not (last and following[0] == G):
                                scores(it, following[0], following[1], pair, t * 2 + (pair + 1))
                            for x in todo[cuts[pair]:cuts[pair + 1]]:
                                side(*x, it)
                        weighted(it, g, s)
                        for x in todo[cuts[2]:]:
                            side(*x, it)

            batches(pe, body)

        def attention_act(act, a):
            ns = a.ns

            def exps(it, g, s, pair, first=False):
                lo = a.steps[s][2]
                t = it * (G * ns) + (g * ns + s)
                act.wait_ge(a.st_full, t * 2 + (pair + 1))
                if not first:
                    act.wait_ge(a.pv_done, t)
                nc.scalar.activation(PR[:, 2 * ((g * ns + s) % 2) + pair, :, lo:CH],
                                     PS[:, 2 * pair:2 * pair + 2, lo:CH], ACT.Exp).then_inc(a.exp_done, 1)

            act.sem_inc(a.ot_free, 1)
            for pair in range(2):
                exps(0, 0, 0, pair, True)

            def body(it, last):
                for g in range(G):
                    for s in range(ns):
                        qc = a.steps[s][0]
                        for pair in range(2):
                            f = (g, s + 1) if s + 1 < ns else (g + 1, 0)
                            if not (last and f[0] == G):
                                exps(it, f[0], f[1], pair)
                        if s + 1 == ns or a.steps[s + 1][0] != qc:
                            t = it * (G * ns) + (g * ns + s)
                            act.wait_ge(a.pv_done, t + 2)
                            act.wait_ge(a.ot_turned, it * (G * NC) + (NC * g + qc + 1))
                            nc.scalar.copy(OT[:, qc, :], PS[:, OT_BANK, :]).then_inc(a.ot_free, 1)

            batches(act, body)

        def attention_dve(dve, a):
            RCHAIN = 5

            def split_max(it, g):
                v = it * G + g
                b2 = g % 2
                mx, mp = MX[:, b2, :, :], MP[:, b2, :, :]
                ops = [lambda: nc.vector.tensor_reduce(NM[:, 0, :], mx, AX_X, ALU.max, negate=True),
                       lambda: nc.vector.tensor_copy(mp[:, 0, :], NM[:, 0, :]),
                       lambda: nc.vector.tensor_tensor(NM[:, 1, :], NM[:, 0, :], mp[:, 0, :], ALU.subtract),
                       lambda: nc.vector.tensor_copy(mp[:, 1, :], NM[:, 1, :])]
                for k, op in enumerate(ops):
                    dve.wait_ge(a.dchain, v * RCHAIN + (k + 1))
                    op().then_inc(a.dchain, 1)
                dve.wait_ge(a.dchain, v * RCHAIN + 5)
                nc.vector.tensor_tensor(mp[:, 2, :], NM[:, 1, :], mp[:, 1, :], ALU.subtract).then_inc(a.parts, 1)

            def side(it, n, slot, item):
                kind = item[0]
                dve.wait_ge(a.sm_full, n + 1)
                bank_ = PS[:, SM_BANK + slot, :]
                if kind == "piece":
                    h, qt, half, width, _ = a.pieces[item[2]]
                    last = item[2] == len(a.pieces) - 1
                    nc.vector.tensor_reduce(MX[:, item[1] % 2, h * KT + qt, half:half + 1], bank_[:, 0:width],
                                            AX_X, ALU.max).then_inc(a.sm_free, 1)
                    if last:
                        dve.wait_ge(a.sm_free, n + 1)
                        dve.sem_inc(a.dchain, 1)
                        split_max(it, item[1])
                elif kind == "rows":
                    nc.vector.tensor_copy(MT[:, item[1] % G, :],
                                          bank_.bitcast(BF16)[0:SPLIT * HG * KT, 0:P]).then_inc(a.sm_free, 1)
                else:
                    g, qc = item[1], item[2]
                    o = NC * g + qc
                    rows = bank_.rearrange("p (t h r) -> p t h r", t=CT, h=HG)
                    rd = RD[:, qc, :].rearrange("p (t h) -> p t h", t=CT)
                    nc.vector.reciprocal(rd, rows[:, :, :, DH]).then_inc(a.ot_turned, 1)
                    dve.wait_ge(a.ot_turned, it * (G * NC) + (o + 3))
                    dst = O[:, bass.ds(it * KT + qc * CT, CT), g * HG * DH:(g + 1) * HG * DH]
                    nc.vector.tensor_tensor(dst.rearrange("p t (h d) -> p t h d", h=HG), rows[:, :, :, 0:DH],
                                            rd.unsqueeze(3).broadcast_to([P, CT, HG, DH]),
                                            ALU.mult).then_inc(a.sm_free, 1)

            dve.sem_inc(a.ot_turned, 2)
            for n, item in enumerate(a.before):
                side(0, n, a.slots_before[n][0], item)

            def body(it, last):
                for g in range(G):
                    for s in range(ns):
                        for n, slot, _, item in a.side(it, last, g, s):
                            side(it, n, slot, item)

            ns = a.ns
            batches(dve, body)

        def attention_pool(pool, a, extra):
            def values(b, g):
                nc.gpsimd.tensor_copy(VR[:, g, :, :].unsqueeze(1),
                                      V[:, bass.ds(b, 1), :, g * HG * VW:(g + 1) * HG * VW]).then_inc(a.values, 1)

            for g in range(G):
                values(0, g)
            extra(pool)
            with pool.Fori(0, B - 1) as it:
                for g in range(G):
                    wait_apart(pool, a.pv_done, it * (G * a.ns) + ((g + 1) * a.ns + 1))
                    values(it + 1, g)

        def attention_sp(sp, a):
            def load(b, g):
                heads = slice(g * HG, (g + 1) * HG)
                for i in range(SPLIT):
                    for j in range(SPLIT):
                        r = (SPLIT * i + j) * DH
                        sp.dma_start(QA[r:r + DH, g, :, :].rearrange("d h t -> d (h t)"),
                                     qs[a.layer][bass.ds(b, 1), i, :, heads, :].rearrange("a d h t -> (a d) (h t)"))\
                            .then_inc(a.loaded[g], 16)
                    r = SPLIT * i * DH
                    sp.dma_start(KA[r:r + SPLIT * DH, g, :, :].rearrange("d h t -> d (h t)"),
                                 ks[a.layer][bass.ds(b, 1), :, :, heads, :].rearrange("a s d h t -> (a s d) (h t)"))\
                        .then_inc(a.loaded[g], 16)

            def maxima(g, n):
                sp.wait_ge(a.sm_free, n + 1)
                for i in range(SPLIT):
                    sp.dma_start(QA[R_MAX + i:R_MAX + i + 1, g, :, :].rearrange("a h (q t) -> a (h q) t", t=P),
                                 MT[i * HG * KT:(i + 1) * HG * KT, g, :]).then_inc(a.maxed[g], 16)

            for g in range(G):
                load(0, g)
            maxima(0, len(a.pieces))

            def body(it, last):
                for g in range(G):
                    for s in range(a.ns):
                        for n, _, _, item in a.side(it, last, g, s):
                            if item[0] == "rows":
                                maxima(item[1] % G, n)
                    if not last:
                        sp.wait_ge(a.exp_done, it * (2 * G * a.ns) + 2 * (g + 1) * a.ns)
                        load(it + 1, g)

            batches(sp, body)

        def butterflies(pool):
            done = [0]

            def settle():
                pool.wait_ge(bfly, done[0])

            def op(dst, a, b, f):
                nc.gpsimd.tensor_tensor(dst, a, b, f).then_inc(bfly, 1)
                done[0] += 1

            def stage(stage, tensors, w, crossed):
                s = 2 ** stage
                wv = w.rearrange("p (n s k) -> p n s k", s=s, k=4)
                for src, dst, rows in tensors:
                    v = src.rearrange("p (n k s) -> p n k s", k=2, s=s)
                    o = dst.rearrange("p (n k s) -> p n k s", k=2, s=s)
                    t = [TMP[0:rows, i, :].rearrange("p (n s) -> p n s", s=s) for i in range(4)]
                    for i, (k, l) in enumerate(((0, 0), (1, 1), (2, 0), (3, 1))):
                        if crossed:
                            k = {0: 0, 1: 2, 2: 1, 3: 3}[k]
                        op(t[i], wv[0:rows, :, :, k], v[0:rows, :, l, :], ALU.mult)
                    settle()
                    op(o[0:rows, :, 0, :], t[0], t[1], ALU.add)
                    op(o[0:rows, :, 1, :], t[2], t[3], ALU.add)
                    settle()

            def load(n):
                src = up_w[n:n + 1, :] if n < STAGES else down_w[2 * STAGES - 1 - n:2 * STAGES - n, :]
                pool.dma_start(WST[:, n % 2, :], src.broadcast_to([P, 4 * HID // 2])).then_inc(bfly_in[n % 2], 16)

            load(0)
            load(1)
            for n in range(2 * STAGES):
                pool.wait_ge(bfly_in[n % 2], 16 * (n // 2 + 1))
                i = n % STAGES
                last = i == STAGES - 1
                if n < STAGES:
                    stage(i, [(YW[:, i % 2, :], WUP[:, :] if last else YW[:, (i + 1) % 2, :], P),
                              (YB[:, i % 2, :], BEFF[:, :] if last else YB[:, (i + 1) % 2, :], 1)],
                          WST[:, n % 2, :], False)
                else:
                    stage(STAGES - 1 - i, [(YC[:, i % 2, :], WDNT[:, :] if last else YC[:, (i + 1) % 2, :], P)],
                          WST[:, n % 2, :], True)
                if n + 2 < 2 * STAGES:
                    load(n + 2)

        @block.sync
        def _(sp):
            for b in range(B):
                sp.dma_start(X[:, b * KT:(b + 1) * KT, :], x[b, :, :].rearrange("(t p) d -> p t d", p=P))\
                    .then_inc(x_in, 16)
            sp.dma_start(ID[:, :], ident).then_inc(x_in, 16)
            sp.dma_start(WQKV[:, :, :], wqkv).then_inc(x_in, 16)
            sp.dma_start(BQK[:, :], bqk).then_inc(x_in, 16)
            sp.dma_start(BV[:, :], bv.broadcast_to([P, D])).then_inc(x_in, 16)
            for g in range(G):
                for h in range(HG):
                    sp.dma_start(KA[R_SPLIT:R_ALL, g, h, :], alibi_k).then_inc(setup, 16)
                sp.dma_start(QA[R_SPLIT:R_MAX, g, :, :], alibi_q[0, :, g * HG:(g + 1) * HG, :]).then_inc(setup, 16)
            for dst, src in ((DIST[:, :, :], dist), (MASK[:, :, :], mask), (IDB[:, :], identb),
                             (DOWN, down_t), (UP[:, :, :], up), (SIGN[:, :], sign.broadcast_to([P, DH])),
                             (COS[:, :], cos), (SIN[:, :], sin), (WOUT[:, 0, :], wout_a), (WOUT[:, 1, :], wout_b),
                             (BOUT[:, :], bout.broadcast_to([P, D])), (UPB[:, :], up_bias),
                             (FB[:, 0, :], b_con.broadcast_to([P, D])), (FB[:, 1, :], down_bias.broadcast_to([P, D]))):
                sp.dma_start(dst, src).then_inc(setup, 16)
            chunks_sp(sp, CA)
            sp.wait_ge(setup, 16 * (G * (HG + 1) + 14))
            end_phase(sp, 1)
            attention_sp(sp, AA)
            end_phase(sp, 2)
            for g in range(G):
                sp.dma_start(QA[R_SPLIT:R_MAX, g, :, :], alibi_q[1, :, g * HG:(g + 1) * HG, :]).then_inc(setup, 16)
            sp.wait_ge(setup, 16 * (G * (HG + 2) + 14))
            end_phase(sp, 3)
            chunks_sp(sp, CB)
            end_phase(sp, 4)
            attention_sp(sp, AB)
            end_phase(sp, 5)
            chunks_sp(sp, CC)

        @block.gpsimd
        def _(pool):
            nc.gpsimd.memset(HALF[:, :], -0.5).then_inc(fold, 1)
            nc.gpsimd.memset(V[:, :, :, :].rearrange("p b k (h w) -> p (b k h) w", w=VW)[:, :, DH:VW], 1.0)
            nc.gpsimd.memset(MX[:, :, :, :], -3.0e38)
            nc.gpsimd.memset(BD[:, :, :, :], 0.0).then_inc(fold, 1)
            pool.wait_ge(fold, 2)
            chunks_pool(pool, CA)
            end_phase(pool, 1)

            def extra(pool):
                nc.gpsimd.tensor_tensor(FB[:, 0, :], FB[:, 0, :], FB[:, 1, :], ALU.add)
                pool.dma_start(YW[:, 0, :], w_exp).then_inc(consts_in, 16)
                pool.dma_start(YB[0:1, 0, :], b_exp).then_inc(consts_in, 16)
                pool.dma_start(YC[:, 0, :], w_con_t).then_inc(consts_in, 16)
                pool.wait_ge(consts_in, 48)
                butterflies(pool)

            attention_pool(pool, AA, extra)
            end_phase(pool, 2)
            nc.gpsimd.memset(MX[:, :, :, :], -3.0e38)
            end_phase(pool, 3)
            chunks_pool(pool, CB)
            end_phase(pool, 4)
            attention_pool(pool, AB, lambda pool: None)
            end_phase(pool, 5)
            chunks_pool(pool, CC)

        @block.scalar
        def _(act):
            chunks_act(act, CA)
            act.wait_ge(folded_pe, 1)
            nc.scalar.copy(WB[:, 0:4, :], PS[:, 0, :].rearrange("p (k d) -> p k d", k=4))
            nc.scalar.copy(WB[:, 4, :], PS[:, 1, 0:P])
            end_phase(act, 1)
            attention_act(act, AA)
            end_phase(act, 2)
            act.wait_ge(folded_pe, 2)
            nc.scalar.copy(WDN[:, :, :], PS[:, 0, :].rearrange("p (n d) -> p n d", n=HC))
            end_phase(act, 3)
            chunks_act(act, CB)
            end_phase(act, 4)
            attention_act(act, AB)
            end_phase(act, 5)
            chunks_act(act, CC)


        @block.vector
        def _(dve):
            dve.wait_ge(x_in, 16 * X_LOADS)
            chunks_dve(dve, CA)
            dve.wait_ge(setup, 16 * (G * (HG + 1) + 14))
            dve.wait_ge(fold, 2)
            for kind in (1, 3):
                s = nc.vector.tensor_tensor(UP[:, kind, :], UP[:, kind, :], SIGN[:, :], ALU.mult)
            s.then_inc(fold, 1)
            dve.wait_ge(fold, 3)
            for half in range(2):
                rows = slice(half * LAT, (half + 1) * LAT)
                s = nc.vector.tensor_copy(BD[rows, :, half, :], UP[rows, :, :])
            s.then_inc(fold, 1)
            end_phase(dve, 1)
            attention_dve(dve, AA)
            end_phase(dve, 2)
            dve.wait_ge(folded_pe, 2)
            nc.vector.tensor_tensor(BUP[:, :], PS[:, 1, 0:HC], UPB[:, :], ALU.add)
            end_phase(dve, 3)
            chunks_dve(dve, CB)
            end_phase(dve, 4)
            attention_dve(dve, AB)
            end_phase(dve, 5)
            chunks_dve(dve, CC)

        @block.tensor
        def _(pe):
            pe.wait_ge(x_in, 16 * X_LOADS)
            chunks_pe(pe, CA)
            pe.wait_ge(CA.turn_free[0], B * CA.turns + 1)
            pe.wait_ge(CA.v_used[0], B + 1)
            pe.wait_ge(fold, 4)
            for kind in range(5):
                for j in range(D // (2 * DH)):
                    to = PS[:, kind // 4, (kind % 4) * P:(kind % 4 + 1) * P]
                    to = to.rearrange("p (d h) -> p h d", h=H) if kind < 4 else to.rearrange("p (h d) -> p h d", h=H)
                    mm = pe.matmul(to[:, 2 * j:2 * j + 2, :],
                                   DOWN[:, (0, 0, 1, 1, 2)[kind], j, :],
                                   BD[:, kind, :, :], start=True, stop=True)
            mm.then_inc(folded_pe, 1)
            end_phase(pe, 1)
            attention_pe(pe, AA)
            end_phase(pe, 2)
            for n in range(HC):
                pe.transpose(PS[:, 0, n * P:(n + 1) * P], WDNT[:, n * P:(n + 1) * P], ID[:, :])
            for n in range(HC):
                mm = pe.matmul(PS[:, 1, n:n + 1], BEFF[0:1, n * P:(n + 1) * P], ID[0:1, 0:1], start=True, stop=True)
            mm.then_inc(folded_pe, 1)
            end_phase(pe, 3)
            chunks_pe(pe, CB)
            end_phase(pe, 4)
            attention_pe(pe, AB)
            end_phase(pe, 5)
            chunks_pe(pe, CC)


def _alibi():
    i = np.arange(T)
    blk, low = i // P, i % P
    slope = 0.5 ** np.arange(H)
    c = np.arange(KT)[:, None]
    far = -np.abs(blk[None] - c) * P
    near = -np.sign(blk[None] - c) * low[None]
    hot = (blk[None] == c).astype(float)
    q = np.stack([far, near, hot]).reshape(R_BIAS, 1, T) * slope[None, :, None]
    q = np.stack([q, 0 * q])
    k = np.concatenate([hot, hot, np.sign(c - blk[None]) * low[None], np.ones((SPLIT, T))])
    j = np.arange(P)
    dist = -np.abs(j[:, None] - j[None])[:, None, :] * slope[None, :, None]
    late = (j[:, None] > j[None]) * -BIG
    mask = np.stack([late, late.T], 1)
    return q, k, dist, mask


def _rope():
    dim = DH // 2
    inv = (np.float32(1.0) / np.float32(10000.0) ** (np.arange(0, dim, 2, dtype=np.float32) / np.float32(dim)))
    freqs = np.arange(T, dtype=np.float32)[:, None] * inv.astype(np.float32)[None, :]
    emb = np.concatenate([freqs, freqs], -1).T
    cos = np.ones((DH, T), np.float32)
    sin = np.zeros((DH, T), np.float32)
    cos[DH // 2:] = np.cos(emb)
    sin[DH // 2:] = np.sin(emb)
    return np.repeat(cos, H, 0), np.repeat(sin, H, 0)


def kernel(**inputs):
    import numpy as np
    import ml_dtypes
    import concourse.bacc as bacc
    from concourse.bass_utils import run_bass_kernel_spmd

    a = {k.removeprefix("L0_"): np.asarray(v) for k, v in inputs.items()}
    bf = ml_dtypes.bfloat16
    q_bias, k_bias, dist, mask = _alibi()
    cos, sin = _rope()
    w, wb = a["attn_a_qkv_w"].reshape(H, 3, DH, D), a["attn_a_qkv_b"].reshape(H, 3, DH)
    qkv = np.stack([w[:, 0].transpose(2, 1, 0).reshape(D, D), w[:, 1].transpose(2, 1, 0).reshape(D, D),
                    w[:, 2].transpose(2, 0, 1).reshape(D, D)], 1)
    qkv_b = np.stack([wb[:, 0].T.reshape(D), wb[:, 1].T.reshape(D), wb[:, 2].reshape(D)])

    def down(name):
        return a[name].T.reshape(D // (2 * DH), P, D).transpose(1, 0, 2)

    def up(c, e):
        return np.concatenate([a[c], a[e]], 1)

    swap = [1, 0, 3, 2]
    q_up, k_up = up("attn_b_Wq_up_c", "attn_b_Wq_up_e"), up("attn_b_Wk_up_c", "attn_b_Wk_up_e")

    def swapped(u):
        return np.concatenate([u[:, :4], u[:, 4:][:, swap]], 1)

    ups = np.stack([q_up, swapped(q_up), k_up, swapped(k_up), a["attn_b_Wv_up"]], 1)
    arrays = {
        "x": a["attn_a_x"], "wqkv": qkv, "bqk": qkv_b[:2].T, "bv": qkv_b[2:3],
        "wout_a": a["attn_a_out_w"].T, "bout": a["attn_a_out_b"][None],
        "ident": np.eye(P, dtype=np.float32), "identb": np.eye(P).astype(bf),
        "alibi_q": q_bias.astype(bf), "alibi_k": k_bias.astype(bf), "dist": dist.astype(bf), "mask": mask.astype(bf),
        "down_t": np.stack([down("attn_b_Wq_down"), down("attn_b_Wk_down"), down("attn_b_Wv_down")], 1),
        "up": np.concatenate([ups, ups]), "sign": np.array([[0, 0, 0, 0, -1, 1, -1, 1]], np.float32),
        "cos": cos, "sin": sin, "wout_b": a["attn_b_Wc"],
        "w_exp": a["ffn_W_exp"], "b_exp": a["ffn_b_exp"][None],
        "up_w": a["ffn_up_weights"].reshape(STAGES, -1), "up_bias": a["ffn_up_bias"].reshape(HC, P).T,
        "down_w": a["ffn_down_weights"].reshape(STAGES, -1), "w_con_t": a["ffn_W_con"].T,
        "b_con": a["ffn_b_con"][None], "down_bias": a["ffn_down_bias"][None],
    }
    arrays = {f"in_{k}": np.ascontiguousarray(v) for k, v in arrays.items()}
    nc = bacc.Bacc("TRN2", target_bir_lowering=False, num_devices=1)
    args = {k[3:]: nc.dram_tensor(k, v.shape, mybir.dt.from_np(v.dtype), kind="ExternalInput").ap()
            for k, v in arrays.items()}
    out = nc.dram_tensor("out", (B, T, D), F32, kind="ExternalOutput").ap()
    build(nc, out=out, **args)
    result = run_bass_kernel_spmd(nc, [arrays], core_ids=[0])
    return result.results[0]["out"]
```

```python
from contextlib import ExitStack

import numpy as np

import concourse.bass as bass
from concourse import mybir

P = 128
B = 4
T = 1024
D = 128
H = 16
DH = D // H
HG = 4
G = H // HG
KT = T // P
CH = 512
CT = CH // P
NC = T // CH
HID = 512
HC = HID // P
STAGES = 9
LAT = 64
VW = DH + 1
SPLIT = 3
R_SPLIT = SPLIT * SPLIT * DH
R_BIAS = 3 * KT
R_MAX = R_SPLIT + R_BIAS
R_ALL = R_MAX + SPLIT
LEAD = 28
ROWS_LAG = 9
LATENCY = 900
EARLY = 2
SIDES = 3
EPS = 1e-5
SCALE = float(np.float32(1.0) / np.sqrt(np.float32(DH)))
BIG = 1e30

F32 = mybir.dt.float32
BF16 = mybir.dt.bfloat16
ALU = mybir.AluOpType
ACT = mybir.ActivationFunctionType
AX_X = mybir.AxisListType.X


def attention_plan(causal):
    steps, pieces = [], []
    for qc in range(NC):
        for kb in range(KT):
            lo = max(0, kb * P - qc * CH) if causal else 0
            if lo < CH:
                steps.append((qc, kb, lo))
    for h in range(HG):
        for qt in range(KT):
            for half in range(NC):
                width = min(CH, (qt + 1) * P - half * CH) if causal else CH
                if width > 0:
                    at = qt * P - half * CH
                    pieces.append((h, qt, half, width, at if 0 <= at < width else None))
    return steps, pieces


def build(nc, x, out, wqkv, bqk, bv, wout_a, bout, ident, identb, alibi_q, alibi_k, dist, mask,
          down_t, up, sign, cos, sin, wout_b, w_exp, b_exp, up_w, up_bias, down_w, w_con_t, b_con,
          down_bias):
    ctx = ExitStack()
    with ctx:
        def sb(name, shape, dt=F32):
            return ctx.enter_context(nc.sbuf_tensor(name, shape, dt))

        def sem(name):
            return ctx.enter_context(nc.semaphore(name))

        def sems(name, n):
            return [sem(f"{name}{i}") for i in range(n)]

        def dram(name, shape, dt):
            return nc.dram_tensor(name, shape, dt, kind="Internal").ap()

        X = sb("X", [P, B * KT, D])
        O = sb("O", [P, B * KT, D])
        V = sb("V", [P, B, KT, H * VW])
        QA = sb("QA", [R_ALL, G, HG, T], BF16)
        KA = sb("KA", [R_ALL, G, HG, T], BF16)
        VR = sb("VR", [P, G, KT, HG * VW])
        DIST = sb("DIST", [P, H, P], BF16)
        MASK = sb("MASK", [P, 2, P], BF16)
        IDB = sb("IDB", [P, P], BF16)
        ID = sb("ID", [P, P])
        MX = sb("MX", [P, 2, HG * KT, NC])
        NM = sb("NM", [P, 3, HG * KT])
        MP = sb("MP", [P, 2, SPLIT, HG * KT], BF16)
        MT = sb("MT", [SPLIT * HG * KT, G, P], BF16)
        OT = sb("OT", [P, NC, CH])
        RD = sb("RD", [P, 2, CT * HG])
        WQKV = sb("WQKV", [P, 3, D])
        BQK = sb("BQK", [P, 2])
        BV = sb("BV", [P, D])
        WOUT = sb("WOUT", [P, 2, D])
        BOUT = sb("BOUT", [P, D])
        WB = sb("WB", [P, 5, D])
        UP = sb("UP", [P, 5, DH])
        SIGN = sb("SIGN", [P, DH])
        BD = sb("BD", [P, 5, 2, DH])
        COS = sb("COS", [P, T])
        SIN = sb("SIN", [P, T])
        WUP = sb("WUP", [P, HID])
        BUP = sb("BUP", [P, HC])
        UPB = sb("UPB", [P, HC])
        WDNT = sb("WDNT", [P, HID])
        WDN = sb("WDN", [P, HC, D])
        BEFF = sb("BEFF", [1, HID])
        FB = sb("FB", [P, 2, D])
        HALF = sb("HALF", [P, CT])
        CHAIN = 10 * CH
        WORK = sb("WORK", [P, 2 * CHAIN])
        ROT = WDNT
        SPL = sb("SPL", [P, 2, 2, SPLIT, CH], BF16)
        STATS = sb("STATS", [P, 2, CT, 6])
        MV = sb("MV", [P, 2, CT, 2])
        VE = sb("VE", [P, 2, CT])
        RS = sb("RS", [P, 2, CT])

        def work(j, at, n=1):
            return WORK[:, j * CHAIN + at * CH:j * CHAIN + (at + n) * CH]

        xn = [work(j, 0) for j in range(2)]
        xt = [work(j, 1) for j in range(2)]
        os_ = [work(j, 2) for j in range(2)]
        ott = [work(j, 3) for j in range(2)]
        gel = [work(j, 4, HC) for j in range(2)]
        q32 = [(work(j, 8), os_[j]) for j in range(2)]
        rest = [(work(j, 9), ott[j]) for j in range(2)]
        PR = WORK[:, 0:4 * 2 * CH].rearrange("p (s h q) -> p s h q", s=4, h=2)
        DOWN = O[:, 0:3 * 8, :].rearrange("p (k j) c -> p k j c", k=3)
        at = 8 * CH
        WST = WORK[:, at:at + 4 * CH].rearrange("p (b w) -> p b w", b=2)
        TMP = WORK[:, at + 4 * CH:at + 6 * CH].rearrange("p (b w) -> p b w", b=4)
        YW = WORK[:, at + 6 * CH:at + 8 * CH].rearrange("p (b w) -> p b w", b=2)
        YB = WORK[:, at + 8 * CH:at + 10 * CH].rearrange("p (b w) -> p b w", b=2)
        YC = WORK[:, at + 10 * CH:at + 12 * CH].rearrange("p (b w) -> p b w", b=2)

        PS = ctx.enter_context(nc.psum_tensor("PS", [P, 8, CH], F32))
        SM_BANK, OT_BANK = 4, 7

        qs = [dram(f"qs{i}", [B, SPLIT, DH, H, T], BF16) for i in range(2)]
        ks = [dram(f"ks{i}", [B, SPLIT, DH, H, T], BF16) for i in range(2)]

        first_in = sem("first_in")
        x_in = sem("x_in")
        ffn_in = sem("ffn_in")
        bias_scaled = sem("bias_scaled")
        phase = sem("phase")
        setup = sem("setup")
        apart = sem("apart")
        fold = sem("fold")
        folded_pe = sem("folded_pe")
        fold_copied = sem("fold_copied")
        bfly_in = sems("bfly_in", 2)
        bfly = sem("bfly")
        out_sem = sem("out_sem")

        block = ctx.enter_context(nc.Block())
        ENGINES = 5
        FIRST_LOADS = 5

        def wait_apart(e, s, value):
            e.wait_ge(s, value)
            e.sem_inc(apart, 1)

        def end_phase(e, n):
            e.drain().then_inc(phase, 1)
            e.wait_ge(phase, ENGINES * n)

        class Chunks:

            def __init__(self, name, layer, attended, ffn, project):
                self.layer, self.attended, self.ffn, self.project = layer, attended, ffn, project
                self.norms = 2 if ffn and project is not None else 1
                self.turns = self.norms + attended
                self.first_wide = HC if ffn else 0
                self.projections = (0 if project is None else (2 if project == 0 else 4))
                self.wides = self.first_wide + self.projections
                self.sums = 2 if project == 1 else 0
                self.splits = 2 if project == 0 else 3
                self.steps = self.sums + 2 * self.splits
                self.lag = 2 if ffn else 1
                self.last_xt = [gel[j][:, 0:CH] if ffn else xt[j] for j in range(2)]

                def two(signal, used=True):
                    return sems(f"{name}_{signal}", 2) if used else None

                self.o_copied = two("o_copied", attended)
                self.x_biased = two("x_biased", attended and layer == 0)
                self.ffn_biased = two("ffn_biased", ffn)
                self.x_added = two("x_added", attended)
                self.stats_done = two("stats_done")
                self.mv_done = two("mv_done")
                self.var_ready = two("var_ready")
                self.rstd_ready = two("rstd_ready")
                self.xn_ready = two("xn_ready")
                self.turn_full = two("turn_full")
                self.turn_free = two("turn_free")
                self.y_full = two("y_full", attended)
                self.y_used = two("y_used", attended)
                self.d_full = two("d_full", ffn)
                self.d_used = two("d_used", ffn)
                self.v_full = two("v_full", project is not None)
                self.v_used = two("v_used", project is not None)
                self.wide_full = two("wide_full")
                self.gelu_done = two("gelu_done", ffn)
                self.proj_used = two("proj_used", project is not None)
                self.split_step = two("split_step", project is not None)
                self.parts_done = two("parts_done", project is not None)
                self.stored = two("stored", project is not None)

        CA = Chunks("pa", 0, 0, 0, 0)
        CB = Chunks("pb", 0, 1, 1, 1)
        CC = Chunks("pc", 1, 1, 1, None)

        def slots(e, c, slot, between=None):
            def at(it, k, lag):
                if isinstance(it, int):
                    n = NC * it + k - lag
                    return divmod(n, NC) if 0 <= n < NC * B else None
                back, j = divmod(k - lag, NC)
                return (it + back if back else it), j

            def batch(it):
                for k in range(NC):
                    where = (at(it, k, 0), at(it, k, 1) if c.ffn else None,
                             at(it, k, c.lag) if c.project is not None else None)
                    if any(w is not None for w in where):
                        slot(*where)

            batch(0)
            with e.Fori(1, B) as it:
                batch(it)
            if between is not None:
                between()
            batch(B)

        def bank(j, i):
            return PS[:, 4 * j + i, :]

        def tile0(it, j):
            return it * KT + j * CT

        def blocks(it, j, n=CT, first=0):
            at = tile0(it, j) + first
            return slice(at, at + n) if isinstance(it, int) else bass.ds(at, n)

        def block_of(it):
            return slice(it, it + 1) if isinstance(it, int) else bass.ds(it, 1)

        def chunks_pe(pe, c):
            def turn(it, j, i, src):
                pe.wait_ge(c.turn_free[j], it * c.turns + (i + 1))
                for t in range(CT):
                    mm = pe.transpose(bank(j, 0)[:, t * P:(t + 1) * P], src[:, t * P:(t + 1) * P], ID[:, :])
                mm.then_inc(c.turn_full[j], 1)

            def normed(it, j, k):
                pe.wait_ge(c.xn_ready[j], it * c.norms + (k + 1))
                turn(it, j, c.attended + k, xn[j])

            def wide(it, j, n, lhs, rhs):
                m, own = (n - 2, 1) if n >= 2 else (n - 2 + c.wides, 0)
                if m < c.first_wide:
                    pe.wait_ge(c.gelu_done[j], it * HC + (own * HC + m + 1))
                else:
                    pe.wait_ge(c.proj_used[j], it * c.projections
                               + (own * c.projections + m - c.first_wide + 1))
                pe.matmul(bank(j, 2 + n % 2), lhs, rhs, start=True, stop=True).then_inc(c.wide_full[j], 1)

            def rows(it, j, src, weights, full):
                for t in range(CT):
                    mm = pe.matmul(bank(j, 1)[:, t * P:(t + 1) * P], src[:, t * P:(t + 1) * P], weights,
                                   start=True, stop=True)
                mm.then_inc(full[j], 1)

            weights, VALUES = (WQKV, 2) if c.project == 0 else (WB, 4)

            def do(part, step, *more):
                if part:
                    step(*part, *more)

            def attended(it, j):
                pe.wait_ge(c.o_copied[j], it + 1)
                turn(it, j, 0, os_[j])

            def out_projection(it, j):
                pe.wait_ge(c.turn_free[j], it * c.turns + 2)
                pe.wait_ge(c.d_used[j], it + 1)
                rows(it, j, ott[j], WOUT[:, c.layer, :], c.y_full)

            def expand(it, j, n):
                if n == 0:
                    pe.wait_ge(c.turn_free[j], it * c.turns + (c.attended + 2))
                wide(it, j, n, WUP[:, n * P:(n + 1) * P], xt[j])

            def contract(it, j, tiles):
                if tiles[0] == 0:
                    if c.v_used is not None:
                        pe.wait_ge(c.v_used[j], it + 1)
                    pe.wait_ge(c.y_used[j], it + 2)
                    pe.wait_ge(c.gelu_done[j], it * HC + 2 * HC)
                for t in tiles:
                    for n in range(HC):
                        mm = pe.matmul(bank(j, 1)[:, t * P:(t + 1) * P],
                                       gel[j][:, n * CH + t * P:n * CH + (t + 1) * P],
                                       WDN[:, n, :], start=(n == 0), stop=(n == HC - 1))
                if tiles[-1] == CT - 1:
                    mm.then_inc(c.d_full[j], 1)

            def project(it, j, k):
                if k == 0:
                    pe.wait_ge(c.turn_free[j], it * c.turns + (c.turns + 1))
                wide(it, j, c.first_wide + k, weights[:, k, :], c.last_xt[j])

            def values(it, j):
                pe.wait_ge(c.v_used[j], it + 1)
                if c.ffn:
                    pe.wait_ge(c.d_used[j], it + 2)
                    if isinstance(it, int) and it == B - 1:
                        pe.wait_ge(c.y_used[j], it + 2)
                    else:
                        pe.wait_ge(c.y_used[j], it + 3)
                rows(it, j, c.last_xt[j], weights[:, VALUES, :], c.v_full)

            def slot(first, second, third):
                if c.project == 0:
                    do(third, project, 0)
                    do(third, project, 1)
                    do(third, values)
                    do(first, normed, 0)
                elif c.project == 1:
                    do(second, expand, 0)
                    do(second, expand, 1)
                    do(second, expand, 2)
                    do(third, normed, 1)
                    do(second, expand, 3)
                    do(first, attended)
                    do(third, project, 0)
                    do(first, out_projection)
                    do(third, project, 1)
                    do(second, contract, range(CT))
                    do(third, project, 2)
                    do(third, project, 3)
                    do(first, normed, 0)
                    do(third, values)
                else:
                    do(second, expand, 0)
                    do(first, attended)
                    do(second, expand, 1)
                    do(second, expand, 2)
                    do(first, out_projection)
                    do(second, expand, 3)
                    do(second, contract, range(CT - 1))
                    do(first, normed, 0)
                    do(second, contract, range(CT - 1, CT))

            for j in range(2):
                for s in (c.y_full, c.d_full, c.v_full):
                    if s is not None:
                        pe.sem_inc(s[j], 1)
            slots(pe, c, slot)

        def chunks_act(act, c):
            def turn(it, j, i, dst, readers):
                act.wait_ge(c.turn_full[j], it * c.turns + (i + 1))
                if readers is not None:
                    act.wait_ge(readers[j], it + 1)
                if c.ffn and c.project is not None and i == 0 and (not isinstance(it, int) or it):
                    act.wait_ge(c.stored[j], it * 32 - 31)
                nc.scalar.copy(dst, bank(j, 0)).then_inc(c.turn_free[j], 1)

            def gelu(it, j, n):
                act.wait_ge(c.wide_full[j], it * c.wides + (n + 1))
                if n == 0:
                    act.wait_ge(c.d_full[j], it + 1)
                    if c.v_full is not None:
                        act.wait_ge(c.v_full[j], it + 1)
                nc.scalar.activation(gel[j][:, n * CH:(n + 1) * CH], bank(j, 2 + n % 2), ACT.Gelu,
                                     bias=BUP[:, n:n + 1]).then_inc(c.gelu_done[j], 1)

            def values(it, j):
                act.wait_ge(c.v_full[j], it + 2)
                nc.scalar.copy(values_of(it, j), bank(j, 1).rearrange("p (t h d) -> p t h d", t=CT, h=H))\
                    .then_inc(c.v_used[j], 1)

            def queries_or_keys(it, j, qk):
                act.wait_ge(c.wide_full[j], it * c.wides + (qk + 1))
                if qk == 0:
                    act.wait_ge(c.stored[j], it * 32 + 1)
                for dst in (q32[j][qk], SPL[:, j, qk, 0, :]):
                    s = nc.scalar.activation(dst, bank(j, 2 + qk), ACT.Identity, bias=BQK[:, qk:qk + 1],
                                             scale=SCALE if qk == 0 else 1.0)
                s.then_inc(c.proj_used[j], 1)

            def gather(it, j):
                if not isinstance(it, int) or it:
                    act.wait_ge(c.turn_free[j], it * c.turns - (c.turns - 2))
                    if c.project is not None:
                        act.wait_ge(c.stored[j], it * 32 - 31)
                nc.scalar.copy(os_[j].rearrange("p (t d) -> p t d", t=CT),
                               O[:, blocks(it, j), :]).then_inc(c.o_copied[j], 1)

            def slot(first, second, third):
                if first and c.attended:
                    gather(*first)
                if c.project == 0:
                    if third:
                        queries_or_keys(*third, 0)
                        queries_or_keys(*third, 1)
                    if first:
                        turn(*first, 0, xt[first[1]], c.v_full)
                    return
                if second:
                    gelu(*second, 0)
                    if c.project == 1:
                        gelu(*second, 1)
                        gelu(*second, 2)
                if third:
                    turn(*third, 2, c.last_xt[third[1]], None)
                if second and c.project == 1:
                    gelu(*second, 3)
                if first:
                    turn(*first, 0, ott[first[1]], c.y_full)
                if second and c.project is None:
                    for n in range(1, HC):
                        gelu(*second, n)
                if first:
                    turn(*first, 1, xt[first[1]], None)
                if third:
                    values(*third)

            for j in range(2):
                act.sem_inc(c.turn_free[j], 1)
                if c.ffn:
                    act.sem_inc(c.gelu_done[j], HC)
                if c.project == 0:
                    act.sem_inc(c.proj_used[j], c.projections)
            slots(act, c, slot)

        def values_of(it, j):
            return V[:, block_of(it), j * CT:(j + 1) * CT, :]\
                .rearrange("p a t (h w) -> p (a t) h w", h=H)[:, :, :, 0:DH]

        def chunks_pool(pool, c):
            def power(it, j, k):
                pool.wait_ge(c.var_ready[j], it * c.norms + (k + 1))
                nc.gpsimd.tensor_tensor(RS[:, j, :], VE[:, j, :], HALF[:, :], ALU.pow).then_inc(c.rstd_ready[j], 1)

            def bias(it, j, row, sem_):
                xs = X[:, blocks(it, j), :]
                nc.gpsimd.tensor_tensor(xs, xs, row.unsqueeze(1).broadcast_to([P, CT, D]),
                                        ALU.add).then_inc(sem_[j], 1)

            def last_part(it, j, qk):
                pool.wait_ge(c.split_step[j], it * c.steps + (c.sums + c.splits * (qk + 1)))
                nc.gpsimd.tensor_tensor(SPL[:, j, qk, 2, :], rest[j][qk], SPL[:, j, qk, 1, :],
                                        ALU.subtract).then_inc(c.parts_done[j], 1)

            def slot(first, second, third):
                if first and c.attended:
                    it, j = first
                    if c.layer == 0:
                        bias(it, j, BOUT[:, :], c.x_biased)
                if first:
                    power(*first, 0)
                if first and c.ffn:
                    it, j = first
                    wait_apart(pool, c.xn_ready[j], it * c.norms + 1)
                    bias(it, j, FB[:, 0, :], c.ffn_biased)
                if second and c.norms == 2:
                    power(*second, 1)
                if third:
                    last_part(*third, 0)
                    last_part(*third, 1)

            if c.project is not None:
                for j in range(2):
                    pool.sem_inc(c.stored[j], 1)
            slots(pool, c, slot)

        def chunks_dve(dve, c):
            adds = c.attended + c.ffn

            def add(it, j, k, full, used, biased):
                dve.wait_ge(full[j], it + 2)
                if biased is not None:
                    dve.wait_ge(biased[j], it + 1)
                xs = X[:, blocks(it, j), :]
                nc.vector.tensor_tensor(xs, bank(j, 1).rearrange("p (t d) -> p t d", t=CT), xs,
                                        ALU.add).then_inc(c.x_added[j], 1)
                dve.wait_ge(c.x_added[j], it * adds + (k + 1))
                dve.sem_inc(used[j], 1)

            def row_of(it, j, t):
                return X[:, blocks(it, j, 1, t), :].rearrange("p a d -> p (a d)")

            def stats(it, j, k):
                if c.project == 0 and not (isinstance(it, int) and it == 0):
                    dve.wait_ge(x_in, 16 * (B - 1))
                for t in range(CT):
                    s = nc.vector.bn_stats(STATS[:, j, t, :], row_of(it, j, t))
                s.then_inc(c.stats_done[j], 1)
                wait_apart(dve, c.stats_done[j], it * c.norms + (k + 1))
                for t in range(CT):
                    s = nc.vector.bn_aggr(MV[:, j, t, :], STATS[:, j, t, :])
                s.then_inc(c.mv_done[j], 1)
                dve.wait_ge(c.mv_done[j], it * c.norms + (k + 1))
                nc.vector.tensor_scalar(VE[:, j, :], MV[:, j, :, 1], EPS, None, ALU.add).then_inc(c.var_ready[j], 1)

            def norm(it, j, k):
                dve.wait_ge(c.rstd_ready[j], it * c.norms + (k + 1))
                dve.wait_ge(c.turn_free[j], it * c.turns + (c.attended + k + 1 if k else 1))
                for t in range(CT):
                    s = nc.vector.tensor_scalar(xn[j][:, t * P:(t + 1) * P], row_of(it, j, t),
                                                MV[:, j, t, 0:1], RS[:, j, t:t + 1], ALU.subtract, ALU.mult)
                s.then_inc(c.xn_ready[j], 1)

            def project(it, j, qk):
                scale = SCALE if qk == 0 else 1.0
                q, r = q32[j][qk], rest[j][qk]
                if qk == 0:
                    dve.wait_ge(c.stored[j], it * 32 + 1)
                cols = slice(j * CH, (j + 1) * CH)
                for i, (dst, table) in enumerate(((r, COS), (ROT[:, :], SIN))):
                    n = c.first_wide + 2 * qk + i
                    if qk == 1 and i == 1:
                        dve.wait_ge(c.split_step[j], it * c.steps + 1)
                    dve.wait_ge(c.wide_full[j], it * c.wides + (n + 1))
                    nc.vector.scalar_tensor_tensor(out=dst, in0=bank(j, 2 + n % 2), scalar=scale,
                                                   in1=table[:, cols], op0=ALU.mult,
                                                   op1=ALU.mult).then_inc(c.proj_used[j], 1)
                dve.wait_ge(c.proj_used[j], it * c.projections + (c.projections + 2 * qk + 2))
                nc.vector.tensor_tensor(q, r, ROT[:, :], ALU.add).then_inc(c.split_step[j], 1)

            def split(it, j, qk):
                q, r = q32[j][qk], rest[j][qk]
                step = it * c.steps + (c.sums + c.splits * qk)
                if c.project == 0:
                    dve.wait_ge(c.proj_used[j], it * c.projections + (c.projections + qk + 1))
                else:
                    dve.wait_ge(c.split_step[j], it * c.steps + (qk + 1))
                    nc.vector.tensor_copy(SPL[:, j, qk, 0, :], q).then_inc(c.split_step[j], 1)
                    dve.wait_ge(c.split_step[j], step + 1)
                nc.vector.tensor_tensor(r, q, SPL[:, j, qk, 0, :], ALU.subtract).then_inc(c.split_step[j], 1)
                dve.wait_ge(c.split_step[j], step + c.splits - 1)
                nc.vector.tensor_copy(SPL[:, j, qk, 1, :], r).then_inc(c.split_step[j], 1)

            def values(it, j):
                dve.wait_ge(c.v_full[j], it + 2)
                nc.vector.tensor_tensor(values_of(it, j), bank(j, 1).rearrange("p (t h d) -> p t h d", t=CT, h=H),
                                        BV[:, :].rearrange("p (h d) -> p h d", h=H).unsqueeze(1)
                                        .broadcast_to([P, CT, H, DH]), ALU.add).then_inc(c.v_used[j], 1)

            def slot(first, second, third):
                if first:
                    if c.attended:
                        add(*first, 0, c.y_full, c.y_used, c.x_biased if c.layer == 0 else None)
                    stats(*first, 0)
                if third:
                    if c.project == 1:
                        project(*third, 0)
                    else:
                        split(*third, 0)
                if first:
                    norm(*first, 0)
                if second:
                    add(*second, 1, c.d_full, c.d_used, c.ffn_biased)
                    if c.norms == 2:
                        stats(*second, 1)
                if third and c.project == 1:
                    project(*third, 1)
                    split(*third, 0)
                if second and c.norms == 2:
                    norm(*second, 1)
                if third:
                    split(*third, 1)
                    if c.project == 0:
                        values(*third)

            for j in range(2):
                for s in (c.y_used, c.d_used, c.v_used):
                    if s is not None:
                        dve.sem_inc(s[j], 1)
                if c.project == 1:
                    dve.sem_inc(c.proj_used[j], c.projections)
            slots(dve, c, slot)

        def chunks_sp(sp, c, following=None):
            def between():
                for j in range(NC):
                    sp.wait_ge(c.stored[j], 32 + 1)
                for g in range(EARLY):
                    load_unit(sp, following, 0, g)

            def slot(first, second, third):
                if c.project is None and second:
                    it, j = second
                    sp.wait_ge(c.x_added[j], it * 2 + 2)
                    sp.dma_start(out[block_of(it), j * CH:(j + 1) * CH, :]
                                 .rearrange("a (t p) d -> p (a t) d", p=P),
                                 X[:, blocks(it, j), :]).then_inc(out_sem, 16)
                if third:
                    it, j = third
                    for qk, scratch in enumerate((qs[c.project], ks[c.project])):
                        sp.wait_ge(c.parts_done[j], it * 2 + (qk + 1))
                        sp.dma_start(scratch[block_of(it), :, :, :, j * CH:(j + 1) * CH]
                                     .rearrange("a s d h t -> (d h) (a s) t"),
                                     SPL[:, j, qk, :, :]).then_inc(c.stored[j], 16)

            slots(sp, c, slot, between if following is not None else None)
            if c.project is None:
                sp.wait_ge(out_sem, 16 * NC * B)

        class Attention:
            def __init__(self, layer):
                self.layer = layer
                self.steps, self.pieces = attention_plan(layer == 1)
                self.ns = len(self.steps)
                self.quota = self.shares()
                n = "ab"[layer]
                self.loaded = sems(f"{n}_loaded", G)
                self.maxed = sems(f"{n}_maxed", G)
                self.values = sem(f"{n}_values")
                self.st_full = sem(f"{n}_st_full")
                self.exp_done = sem(f"{n}_exp_done")
                self.pv_done = sem(f"{n}_pv_done")
                self.ot_free = sem(f"{n}_ot_free")
                self.ot_turned = sem(f"{n}_ot_turned")
                self.sm_full = sem(f"{n}_sm_full")
                self.sm_free = sem(f"{n}_sm_free")
                self.parts = sem(f"{n}_parts")
                self.dchain = sem(f"{n}_dchain")
                self.before = [("piece", 0, i) for i in range(len(self.pieces))]
                self.before += [("piece", 1, i) for i in range(ROWS_LAG)] + [("rows", 0)]
                self.before += [("piece", 1, i) for i in range(ROWS_LAG, LEAD)]
                self.base = len(self.before)
                self.steady = [(g, s, x) for g in range(G) for s in range(self.ns) for x in self.items(g, s)]
                self.total = len(self.steady)
                self.final = [y for y in self.steady if y[2][0] == "out" or y[2][1] < G]
                steady = [k % SIDES for k in range(self.total)]
                before = steady[-self.base:]
                self.slots_before = self.distances([], before)
                self.slots_steady = self.distances(steady, steady)
                self.slots_final = self.distances(steady, steady[:len(self.final)])

            def distances(self, history, slots):
                whole = history + slots
                result = []
                for k in range(len(history), len(whole)):
                    d = next((d for d in range(1, k + 1) if whole[k - d] == whole[k]), None)
                    result.append((whole[k], d))
                return result

            def shares(self):
                n = len(self.pieces)
                cost = [self.pieces[(i + LEAD) % n][3] + 64 for i in range(n)]
                weight = [(CH - lo) * 2 + (256 if 0 <= kb * P - qc * CH < CH else 0) + LATENCY
                          for qc, kb, lo in self.steps]
                quota, i, spent, done = [], 0, 0, 0
                for w in weight:
                    done += w
                    first = i
                    while i < n and spent + cost[i] / 2 < sum(cost) * done / sum(weight):
                        spent += cost[i]
                        i += 1
                    quota.append(i - first)
                quota[-1] += n - i
                return quota

            def items(self, g, s):
                n = len(self.pieces)
                first = g * n + sum(self.quota[:s]) + LEAD
                items = []
                for p in range(first, first + self.quota[s]):
                    items.append(("piece", p // n + 1, p % n))
                    if p % n == ROWS_LAG - 1:
                        items.append(("rows", p // n))
                half = next(i for i, (qc, _, _) in enumerate(self.steps) if qc == 1)
                if s == half + 3:
                    items.append(("out", g, 0))
                if g and s == 2:
                    items.append(("out", g - 1, 1))
                if g == G - 1 and s == self.ns - 1:
                    items.append(("out", g, 1))
                return items

            def side(self, it, last, g, s):
                items, slots = (self.final, self.slots_final) if last else (self.steady, self.slots_steady)
                return [(it * self.total + (self.base + k), slots[k][0], slots[k][1], x)
                        for k, (gg, ss, x) in enumerate(items) if (gg, ss) == (g, s)]

        AA, AB = Attention(0), Attention(1)

        def batches(e, body):
            with e.Fori(0, B - 1) as it:
                body(it, False)
            body(B - 1, True)

        def unit_of(it, g):
            return (it, g) if g < G else (it + 1, g - G)

        def attention_pe(pe, a):
            ns = a.ns

            def scores(it, g, s, pair, m):
                b, g = unit_of(it, g)
                qc, kb, lo = a.steps[s]
                if s == 0 and pair == 0:
                    pe.wait_ge(a.maxed[g], (b + 1) * 48)
                if m is not None:
                    pe.wait_ge(a.exp_done, m)
                for hh in range(2):
                    h = 2 * pair + hh
                    diagonal = kb * P - qc * CH
                    has = 0 <= diagonal < CH
                    mm = pe.matmul(PS[:, 2 * pair + hh, lo:CH], KA[:, g, h, kb * P:(kb + 1) * P],
                                   QA[:, g, h, qc * CH + lo:(qc + 1) * CH], start=True, stop=not has)
                    if has:
                        block = DIST[:, g * HG + h, :] if a.layer == 0 else MASK[:, 0, :]
                        mm = pe.matmul(PS[:, 2 * pair + hh, diagonal:diagonal + P], IDB[:, :], block,
                                       start=False, stop=True)
                mm.then_inc(a.st_full, 1)

            def weighted(it, g, s):
                qc, kb, lo = a.steps[s]
                t = it * (G * ns) + (g * ns + s)
                if s == 0:
                    pe.wait_ge(a.values, it * G + (g + 1))
                if kb == 0:
                    pe.wait_ge(a.ot_free, it * (G * NC) + (NC * g + qc + 1))
                pe.wait_ge(a.exp_done, t * 2 + 2)
                last = s + 1 == ns or a.steps[s + 1][0] != qc
                for h in range(HG):
                    mm = pe.matmul(PS[32 * h:32 * h + VW, OT_BANK, lo:CH],
                                   VR[:, g, kb, h * VW:(h + 1) * VW],
                                   PR[:, 2 * ((g * ns + s) % 2) + h // 2, h % 2, lo:CH],
                                   start=(kb == 0), stop=last)
                mm.then_inc(a.pv_done, 1)

            def side(n, slot, back, item, it=0):
                kind = item[0]
                if back is not None:
                    pe.wait_ge(a.sm_free, n - (back - 1))
                bank_ = PS[:, SM_BANK + slot, :]
                if kind == "piece":
                    b, g = unit_of(it, item[1])
                    h, qt, half, width, diagonal = a.pieces[item[2]]
                    if item[2] == 0:
                        pe.wait_ge(a.loaded[g], (b + 1) * 16 * (SPLIT + 1))
                    mm = pe.matmul(bank_[:, 0:width], QA[0:R_MAX, g, h, qt * P:(qt + 1) * P],
                                   KA[0:R_MAX, g, h, half * CH:half * CH + width],
                                   start=True, stop=diagonal is None)
                    if diagonal is not None:
                        block = DIST[:, g * HG + h, :] if a.layer == 0 else MASK[:, 1, :]
                        mm = pe.matmul(bank_[:, diagonal:diagonal + P], IDB[:, :], block, start=False, stop=True)
                elif kind == "rows":
                    pe.wait_ge(a.parts, it * G + (item[1] + 1))
                    mm = pe.transpose(bank_.bitcast(BF16)[0:SPLIT * HG * KT, 0:P],
                                      MP[:, item[1] % 2, :, :].rearrange("p s r -> p (s r)"), IDB[:, :])
                else:
                    o = NC * item[1] + item[2]
                    pe.wait_ge(a.ot_free, it * (G * NC) + (o + 2))
                    for t in range(CT):
                        mm = pe.transpose(bank_[:, t * P:(t + 1) * P], OT[:, item[2], t * P:(t + 1) * P], ID[:, :])
                mm.then_inc(a.sm_full, 1)

            pe.sem_inc(a.pv_done, 1)
            for n, item in enumerate(a.before):
                side(n, *a.slots_before[n], item)
            if a.layer == 0:
                pe.wait_ge(fold_copied, 1)
            for pair in range(2):
                scores(0, 0, 0, pair, None)

            def body(it, last):
                for g in range(G):
                    for s in range(ns):
                        todo = a.side(it, last, g, s)
                        following = (g, s + 1) if s + 1 < ns else (g + 1, 0)
                        t = it * (G * ns) + (g * ns + s)
                        cuts = [len(todo) * i // (4 if a.layer == 0 else 3) for i in range(3)]
                        for pair in range(2):
                            if not (last and following[0] == G):
                                scores(it, following[0], following[1], pair, t * 2 + (pair + 1))
                            for x in todo[cuts[pair]:cuts[pair + 1]]:
                                side(*x, it)
                        weighted(it, g, s)
                        for x in todo[cuts[2]:]:
                            side(*x, it)

            batches(pe, body)

        def attention_act(act, a):
            ns = a.ns

            def exps(it, g, s, pair, first=False):
                lo = a.steps[s][2]
                t = it * (G * ns) + (g * ns + s)
                act.wait_ge(a.st_full, t * 2 + (pair + 1))
                if not first:
                    act.wait_ge(a.pv_done, t)
                nc.scalar.activation(PR[:, 2 * ((g * ns + s) % 2) + pair, :, lo:CH],
                                     PS[:, 2 * pair:2 * pair + 2, lo:CH], ACT.Exp).then_inc(a.exp_done, 1)

            act.sem_inc(a.ot_free, 1)
            for pair in range(2):
                exps(0, 0, 0, pair, True)

            def body(it, last):
                for g in range(G):
                    for s in range(ns):
                        qc = a.steps[s][0]
                        for pair in range(2):
                            f = (g, s + 1) if s + 1 < ns else (g + 1, 0)
                            if not (last and f[0] == G):
                                exps(it, f[0], f[1], pair)
                        if s + 1 == ns or a.steps[s + 1][0] != qc:
                            t = it * (G * ns) + (g * ns + s)
                            act.wait_ge(a.pv_done, t + 2)
                            act.wait_ge(a.ot_turned, it * (G * NC) + (NC * g + qc + 1))
                            nc.scalar.copy(OT[:, qc, :], PS[:, OT_BANK, :]).then_inc(a.ot_free, 1)

            batches(act, body)

        def attention_dve(dve, a):
            def split_max(it, g, k, n):
                v = it * G + g
                mx, mp = MX[:, g % 2, :, :], MP[:, g % 2, :, :]
                if k == 0:
                    dve.wait_ge(a.sm_free, n)
                    dve.sem_inc(a.dchain, 1)
                dve.wait_ge(a.dchain, v * 5 + (k + 1))
                if k == 0:
                    nc.vector.tensor_reduce(NM[:, 0, :], mx, AX_X, ALU.max, negate=True).then_inc(a.dchain, 1)
                elif k == 1:
                    nc.vector.tensor_copy(mp[:, 0, :], NM[:, 0, :]).then_inc(a.dchain, 1)
                elif k == 2:
                    nc.vector.tensor_tensor(NM[:, 1, :], NM[:, 0, :], mp[:, 0, :], ALU.subtract).then_inc(a.dchain, 1)
                elif k == 3:
                    nc.vector.tensor_copy(mp[:, 1, :], NM[:, 1, :]).then_inc(a.dchain, 1)
                else:
                    nc.vector.tensor_tensor(mp[:, 2, :], NM[:, 1, :], mp[:, 1, :], ALU.subtract).then_inc(a.parts, 1)

            def side(it, n, slot, item, last=False):
                kind = item[0]
                dve.wait_ge(a.sm_full, n + 1)
                bank_ = PS[:, SM_BANK + slot, :]
                if kind == "piece":
                    h, qt, half, width, _ = a.pieces[item[2]]
                    nc.vector.tensor_reduce(MX[:, item[1] % 2, h * KT + qt, half:half + 1], bank_[:, 0:width],
                                            AX_X, ALU.max).then_inc(a.sm_free, 1)
                    if item[1] and item[2] < 5:
                        split_max(it, item[1] - 1, item[2], n)
                    if last and item[1] == G - 1 and item[2] == len(a.pieces) - 1:
                        for k in range(5):
                            split_max(it, item[1], k, n + 1)
                elif kind == "rows":
                    nc.vector.tensor_copy(MT[:, item[1] % G, :],
                                          bank_.bitcast(BF16)[0:SPLIT * HG * KT, 0:P]).then_inc(a.sm_free, 1)
                else:
                    g, qc = item[1], item[2]
                    o = NC * g + qc
                    rows = bank_.rearrange("p (t h r) -> p t h r", t=CT, h=HG)
                    rd = RD[:, qc, :].rearrange("p (t h) -> p t h", t=CT)
                    nc.vector.reciprocal(rd, rows[:, :, :, DH]).then_inc(a.ot_turned, 1)
                    dve.wait_ge(a.ot_turned, it * (G * NC) + (o + 3))
                    dst = O[:, bass.ds(it * KT + qc * CT, CT), g * HG * DH:(g + 1) * HG * DH]
                    nc.vector.tensor_tensor(dst.rearrange("p t (h d) -> p t h d", h=HG), rows[:, :, :, 0:DH],
                                            rd.unsqueeze(3).broadcast_to([P, CT, HG, DH]),
                                            ALU.mult).then_inc(a.sm_free, 1)

            dve.sem_inc(a.ot_turned, 2)
            for n, item in enumerate(a.before):
                side(0, n, a.slots_before[n][0], item)

            def body(it, last):
                for g in range(G):
                    for s in range(ns):
                        for n, slot, _, item in a.side(it, last, g, s):
                            side(it, n, slot, item, last)

            ns = a.ns
            batches(dve, body)

        def attention_pool(pool, a, extra):
            def values(b, g):
                nc.gpsimd.tensor_copy(VR[:, g, :, :].unsqueeze(1),
                                      V[:, bass.ds(b, 1), :, g * HG * VW:(g + 1) * HG * VW]).then_inc(a.values, 1)

            for g in range(G):
                values(0, g)
            extra(pool)
            with pool.Fori(0, B - 1) as it:
                for g in range(G):
                    wait_apart(pool, a.pv_done, it * (G * a.ns) + ((g + 1) * a.ns + 1))
                    values(it + 1, g)

        def load_unit(sp, a, b, g):
            heads = slice(g * HG, (g + 1) * HG)
            for i in range(SPLIT):
                sp.dma_start(QA[SPLIT * i * DH:SPLIT * (i + 1) * DH, g, :, :].rearrange("r h t -> r (h t)"),
                             qs[a.layer][bass.ds(b, 1), i, :, heads, :].rearrange("a d h t -> a d (h t)")
                             .broadcast_to([SPLIT, DH, HG * T])).then_inc(a.loaded[g], 16)
            sp.dma_start(KA[0:R_SPLIT, g, :, :].rearrange("r h t -> r (h t)"),
                         ks[a.layer][bass.ds(b, 1), :, :, heads, :].rearrange("a s d h t -> a (s d) (h t)")
                         .broadcast_to([SPLIT, SPLIT * DH, HG * T])).then_inc(a.loaded[g], 16)

        def attention_sp(sp, a, before, n):
            def maxima(g, item):
                sp.wait_ge(a.sm_free, item + 1)
                for i in range(SPLIT):
                    sp.dma_start(QA[R_MAX + i:R_MAX + i + 1, g, :, :].rearrange("a h (q t) -> a (h q) t", t=P),
                                 MT[i * HG * KT:(i + 1) * HG * KT, g, :]).then_inc(a.maxed[g], 16)

            sp.drain().then_inc(phase, 1)
            for j in range(NC):
                sp.wait_ge(before.stored[j], 32 * B + 1)
            for g in range(EARLY, G):
                load_unit(sp, a, 0, g)
            sp.wait_ge(phase, ENGINES * n)
            maxima(0, a.before.index(("rows", 0)))

            def body(it, last):
                for g in range(G):
                    for s in range(a.ns):
                        for number, _, _, item in a.side(it, last, g, s):
                            if item[0] == "rows":
                                maxima(item[1] % G, number)
                    if not last:
                        sp.wait_ge(a.exp_done, it * (2 * G * a.ns) + 2 * (g + 1) * a.ns)
                        load_unit(sp, a, it + 1, g)

            batches(sp, body)

        def butterflies(pool):
            done = [0]

            def settle():
                pool.wait_ge(bfly, done[0])

            def op(dst, a, b, f):
                nc.gpsimd.tensor_tensor(dst, a, b, f).then_inc(bfly, 1)
                done[0] += 1

            def stage(stage, tensors, w, crossed):
                s = 2 ** stage
                wv = w.rearrange("p (n s k) -> p n s k", s=s, k=4)
                for src, dst, rows in tensors:
                    v = src.rearrange("p (n k s) -> p n k s", k=2, s=s)
                    o = dst.rearrange("p (n k s) -> p n k s", k=2, s=s)
                    t = [TMP[0:rows, i, :].rearrange("p (n s) -> p n s", s=s) for i in range(4)]
                    for i, (k, l) in enumerate(((0, 0), (1, 1), (2, 0), (3, 1))):
                        if crossed:
                            k = {0: 0, 1: 2, 2: 1, 3: 3}[k]
                        op(t[i], wv[0:rows, :, :, k], v[0:rows, :, l, :], ALU.mult)
                    settle()
                    op(o[0:rows, :, 0, :], t[0], t[1], ALU.add)
                    op(o[0:rows, :, 1, :], t[2], t[3], ALU.add)
                    settle()

            def load(n):
                src = up_w[n:n + 1, :] if n < STAGES else down_w[2 * STAGES - 1 - n:2 * STAGES - n, :]
                pool.dma_start(WST[:, n % 2, :], src.broadcast_to([P, 4 * HID // 2])).then_inc(bfly_in[n % 2], 16)

            load(0)
            load(1)
            for n in range(2 * STAGES):
                pool.wait_ge(bfly_in[n % 2], 16 * (n // 2 + 1))
                i = n % STAGES
                last = i == STAGES - 1
                if n < STAGES:
                    stage(i, [(YW[:, i % 2, :], WUP[:, :] if last else YW[:, (i + 1) % 2, :], P),
                              (YB[:, i % 2, :], BEFF[:, :] if last else YB[:, (i + 1) % 2, :], 1)],
                          WST[:, n % 2, :], False)
                else:
                    stage(STAGES - 1 - i, [(YC[:, i % 2, :], WDNT[:, :] if last else YC[:, (i + 1) % 2, :], P)],
                          WST[:, n % 2, :], True)
                if n + 2 < 2 * STAGES:
                    load(n + 2)

        @block.sync
        def _(sp):
            for b in range(B):
                sp.dma_start(X[:, b * KT:(b + 1) * KT, :], x[b, :, :].rearrange("(t p) d -> p t d", p=P))\
                    .then_inc(x_in if b else first_in, 16)
                if b == 0:
                    for dst, src in ((ID[:, :], ident), (WQKV[:, :, :], wqkv), (BQK[:, :], bqk),
                                     (BV[:, :], bv.broadcast_to([P, D]))):
                        sp.dma_start(dst, src).then_inc(first_in, 16)
            for g in range(G):
                for h in range(HG):
                    sp.dma_start(KA[R_SPLIT:R_ALL, g, h, :], alibi_k).then_inc(setup, 16)
                sp.dma_start(QA[R_SPLIT:R_MAX, g, :, :], alibi_q[0, :, g * HG:(g + 1) * HG, :]).then_inc(setup, 16)
            for dst, src in ((DIST[:, :, :], dist), (MASK[:, :, :], mask), (IDB[:, :], identb),
                             (DOWN, down_t), (UP[:, :, :], up), (SIGN[:, :], sign.broadcast_to([P, DH])),
                             (COS[:, :], cos), (SIN[:, :], sin), (WOUT[:, 0, :], wout_a), (WOUT[:, 1, :], wout_b),
                             (BOUT[:, :], bout.broadcast_to([P, D])), (UPB[:, :], up_bias),
                             (FB[:, 0, :], b_con.broadcast_to([P, D])), (FB[:, 1, :], down_bias.broadcast_to([P, D]))):
                sp.dma_start(dst, src).then_inc(setup, 16)
            chunks_sp(sp, CA, AA)
            sp.wait_ge(setup, 16 * (G * (HG + 1) + 14))
            attention_sp(sp, AA, CA, 1)
            end_phase(sp, 2)
            for g in range(G):
                sp.dma_start(QA[R_SPLIT:R_MAX, g, :, :], alibi_q[1, :, g * HG:(g + 1) * HG, :]).then_inc(setup, 16)
            chunks_sp(sp, CB, AB)
            sp.wait_ge(setup, 16 * (G * (HG + 2) + 14))
            attention_sp(sp, AB, CB, 3)
            end_phase(sp, 4)
            chunks_sp(sp, CC)

        @block.gpsimd
        def _(pool):
            nc.gpsimd.memset(HALF[:, :], -0.5).then_inc(fold, 1)
            nc.gpsimd.memset(V[:, :, :, :].rearrange("p b k (h w) -> p (b k h) w", w=VW)[:, :, DH:VW], 1.0)
            nc.gpsimd.memset(MX[:, :, :, :], -3.0e38)
            nc.gpsimd.memset(BD[:, :, :, :], 0.0).then_inc(fold, 1)
            pool.wait_ge(fold, 2)
            chunks_pool(pool, CA)
            end_phase(pool, 1)

            def extra(pool):
                nc.gpsimd.tensor_tensor(FB[:, 0, :], FB[:, 0, :], FB[:, 1, :], ALU.add)
                pool.dma_start(YW[:, 0, :], w_exp).then_inc(ffn_in, 16)
                pool.dma_start(YB[0:1, 0, :], b_exp).then_inc(ffn_in, 16)
                pool.dma_start(YC[:, 0, :], w_con_t).then_inc(ffn_in, 16)
                pool.wait_ge(ffn_in, 48)
                butterflies(pool)

            attention_pool(pool, AA, extra)
            end_phase(pool, 2)
            nc.gpsimd.memset(MX[:, :, :, :], -3.0e38)
            chunks_pool(pool, CB)
            end_phase(pool, 3)
            attention_pool(pool, AB, lambda pool: None)
            end_phase(pool, 4)
            chunks_pool(pool, CC)

        @block.scalar
        def _(act):
            act.wait_ge(first_in, 16 * FIRST_LOADS)
            nc.scalar.activation(BQK[:, 0:1], BQK[:, 0:1], ACT.Copy, scale=SCALE).then_inc(bias_scaled, 1)
            act.wait_ge(bias_scaled, 1)
            chunks_act(act, CA)
            end_phase(act, 1)
            act.wait_ge(folded_pe, 1)
            nc.scalar.copy(WB[:, 0:4, :], PS[:, 0, :].rearrange("p (k d) -> p k d", k=4))
            nc.scalar.copy(WB[:, 4, :], PS[:, 1, 0:P]).then_inc(fold_copied, 1)
            attention_act(act, AA)
            end_phase(act, 2)
            act.wait_ge(folded_pe, 2)
            nc.scalar.copy(WDN[:, :, :], PS[:, 0, :].rearrange("p (n d) -> p n d", n=HC)).then_inc(fold_copied, 1)
            act.wait_ge(fold_copied, 3)
            chunks_act(act, CB)
            end_phase(act, 3)
            attention_act(act, AB)
            end_phase(act, 4)
            chunks_act(act, CC)


        @block.vector
        def _(dve):
            dve.wait_ge(first_in, 16 * FIRST_LOADS)
            chunks_dve(dve, CA)
            dve.wait_ge(setup, 16 * (G * (HG + 1) + 14))
            dve.wait_ge(fold, 2)
            for kind in (1, 3):
                s = nc.vector.tensor_tensor(UP[:, kind, :], UP[:, kind, :], SIGN[:, :], ALU.mult)
            s.then_inc(fold, 1)
            dve.wait_ge(fold, 3)
            for half in range(2):
                rows = slice(half * LAT, (half + 1) * LAT)
                s = nc.vector.tensor_copy(BD[rows, :, half, :], UP[rows, :, :])
            s.then_inc(fold, 1)
            end_phase(dve, 1)
            attention_dve(dve, AA)
            end_phase(dve, 2)
            dve.wait_ge(folded_pe, 2)
            nc.vector.tensor_tensor(BUP[:, :], PS[:, 1, 0:HC], UPB[:, :], ALU.add).then_inc(fold_copied, 1)
            chunks_dve(dve, CB)
            end_phase(dve, 3)
            attention_dve(dve, AB)
            end_phase(dve, 4)
            chunks_dve(dve, CC)

        @block.tensor
        def _(pe):
            pe.wait_ge(first_in, 16 * FIRST_LOADS)
            chunks_pe(pe, CA)
            end_phase(pe, 1)

            pe.wait_ge(fold, 4)
            for k in range(3):
                for j in range(D // (2 * DH)):
                    if k < 2:
                        kinds = slice(2 * k, 2 * k + 2)
                        to = PS[:, 0, 2 * k * P:2 * (k + 1) * P].rearrange("p (k d h) -> p k h d", k=2, h=H)
                    else:
                        kinds = slice(4, 5)
                        to = PS[:, 1, 0:P].rearrange("p (k h d) -> p k h d", k=1, h=H)
                    mm = pe.matmul(to[:, :, 2 * j:2 * j + 2, :], DOWN[:, k, j, :], BD[:, kinds, :, :],
                                   start=True, stop=True)
            mm.then_inc(folded_pe, 1)
            attention_pe(pe, AA)
            end_phase(pe, 2)
            for n in range(HC):
                pe.transpose(PS[:, 0, n * P:(n + 1) * P], WDNT[:, n * P:(n + 1) * P], ID[:, :])
            for n in range(HC):
                mm = pe.matmul(PS[:, 1, n:n + 1], BEFF[0:1, n * P:(n + 1) * P], ID[0:1, 0:1], start=True, stop=True)
            mm.then_inc(folded_pe, 1)
            pe.wait_ge(fold_copied, 3)
            chunks_pe(pe, CB)
            end_phase(pe, 3)
            attention_pe(pe, AB)
            end_phase(pe, 4)
            chunks_pe(pe, CC)


def _alibi():
    i = np.arange(T)
    blk, low = i // P, i % P
    slope = 0.5 ** np.arange(H)
    c = np.arange(KT)[:, None]
    far = -np.abs(blk[None] - c) * P
    near = -np.sign(blk[None] - c) * low[None]
    hot = (blk[None] == c).astype(float)
    q = np.stack([far, near, hot]).reshape(R_BIAS, 1, T) * slope[None, :, None]
    q = np.stack([q, 0 * q])
    k = np.concatenate([hot, hot, np.sign(c - blk[None]) * low[None], np.ones((SPLIT, T))])
    j = np.arange(P)
    dist = -np.abs(j[:, None] - j[None])[:, None, :] * slope[None, :, None]
    late = (j[:, None] > j[None]) * -BIG
    mask = np.stack([late, late.T], 1)
    return q, k, dist, mask


def _rope():
    dim = DH // 2
    inv = (np.float32(1.0) / np.float32(10000.0) ** (np.arange(0, dim, 2, dtype=np.float32) / np.float32(dim)))
    freqs = np.arange(T, dtype=np.float32)[:, None] * inv.astype(np.float32)[None, :]
    emb = np.concatenate([freqs, freqs], -1).T
    cos = np.ones((DH, T), np.float32)
    sin = np.zeros((DH, T), np.float32)
    cos[DH // 2:] = np.cos(emb)
    sin[DH // 2:] = np.sin(emb)
    return np.repeat(cos, H, 0), np.repeat(sin, H, 0)


def kernel(**inputs):
    import numpy as np
    import ml_dtypes
    import concourse.bacc as bacc
    from concourse.bass_utils import run_bass_kernel_spmd

    a = {k.removeprefix("L0_"): np.asarray(v) for k, v in inputs.items()}
    bf = ml_dtypes.bfloat16
    q_bias, k_bias, dist, mask = _alibi()
    cos, sin = _rope()
    w, wb = a["attn_a_qkv_w"].reshape(H, 3, DH, D), a["attn_a_qkv_b"].reshape(H, 3, DH)
    qkv = np.stack([w[:, 0].transpose(2, 1, 0).reshape(D, D), w[:, 1].transpose(2, 1, 0).reshape(D, D),
                    w[:, 2].transpose(2, 0, 1).reshape(D, D)], 1)
    qkv_b = np.stack([wb[:, 0].T.reshape(D), wb[:, 1].T.reshape(D), wb[:, 2].reshape(D)])

    def down(name):
        return a[name].T.reshape(D // (2 * DH), P, D).transpose(1, 0, 2)

    def up(c, e):
        return np.concatenate([a[c], a[e]], 1)

    swap = [1, 0, 3, 2]
    q_up, k_up = up("attn_b_Wq_up_c", "attn_b_Wq_up_e"), up("attn_b_Wk_up_c", "attn_b_Wk_up_e")

    def swapped(u):
        return np.concatenate([u[:, :4], u[:, 4:][:, swap]], 1)

    ups = np.stack([q_up, swapped(q_up), k_up, swapped(k_up), a["attn_b_Wv_up"]], 1)
    arrays = {
        "x": a["attn_a_x"], "wqkv": qkv, "bqk": qkv_b[:2].T, "bv": qkv_b[2:3],
        "wout_a": a["attn_a_out_w"].T, "bout": a["attn_a_out_b"][None],
        "ident": np.eye(P, dtype=np.float32), "identb": np.eye(P).astype(bf),
        "alibi_q": q_bias.astype(bf), "alibi_k": k_bias.astype(bf), "dist": dist.astype(bf), "mask": mask.astype(bf),
        "down_t": np.stack([down("attn_b_Wq_down"), down("attn_b_Wk_down"), down("attn_b_Wv_down")], 1),
        "up": np.concatenate([ups, ups]), "sign": np.array([[0, 0, 0, 0, -1, 1, -1, 1]], np.float32),
        "cos": cos, "sin": sin, "wout_b": a["attn_b_Wc"],
        "w_exp": a["ffn_W_exp"], "b_exp": a["ffn_b_exp"][None],
        "up_w": a["ffn_up_weights"].reshape(STAGES, -1), "up_bias": a["ffn_up_bias"].reshape(HC, P).T,
        "down_w": a["ffn_down_weights"].reshape(STAGES, -1), "w_con_t": a["ffn_W_con"].T,
        "b_con": a["ffn_b_con"][None], "down_bias": a["ffn_down_bias"][None],
    }
    arrays = {f"in_{k}": np.ascontiguousarray(v) for k, v in arrays.items()}
    nc = bacc.Bacc("TRN2", target_bir_lowering=False, num_devices=1)
    args = {k[3:]: nc.dram_tensor(k, v.shape, mybir.dt.from_np(v.dtype), kind="ExternalInput").ap()
            for k, v in arrays.items()}
    out = nc.dram_tensor("out", (B, T, D), F32, kind="ExternalOutput").ap()
    build(nc, out=out, **args)
    result = run_bass_kernel_spmd(nc, [arrays], core_ids=[0])
    return result.results[0]["out"]
```
